# Optimizing a Trainium2 kernel written in Bass

```python
import numpy as np
import jax
import jax.numpy as jnp

def _softmax(x, axis=-1):
    return jax.nn.softmax(x, axis=axis)

def _gelu(x):
    return jax.nn.gelu(x, approximate=True)

def _silu(x):
    return jax.nn.silu(x)

def _sigmoid(x):
    return jax.nn.sigmoid(x)

def _layernorm(x, axis=-1, eps=1e-05):
    m = jnp.mean(x, axis=axis, keepdims=True)
    v = jnp.var(x, axis=axis, keepdims=True)
    return (x - m) / jnp.sqrt(v + eps)

def _scatter_add(tgt, idx, src, axis=0):
    return tgt.at[idx].add(src)

def _segment_sum(src, seg, n):
    return jax.ops.segment_sum(src, seg, n)
kernel_name = 'mk_macaron_d1_jaxref_r8_032874'

def setup_inputs(seed: int=0):
    np.random.seed(seed)
    _w = jnp.asarray

    def _L0_attn_setup():
        import jax, jax.numpy as jnp
        import numpy as np
        BATCH, SEQ, D_MODEL, N_HEADS, D_HEAD = (2, 256, 256, 16, 128)
        ATTN_SCALE = np.sqrt(D_HEAD).astype(np.float32)
        IGNORE = jnp.float32(-100000.0)
        key = jax.random.key(seed)
        ks = jax.random.split(key, 5)
        init = 1.0 / np.sqrt(D_MODEL)
        return {'x': jax.random.normal(ks[0], (BATCH, SEQ, D_MODEL), jnp.float32), 'W_Q': jax.random.normal(ks[1], (N_HEADS, D_MODEL, D_HEAD), jnp.float32) * init, 'W_K': jax.random.normal(ks[2], (N_HEADS, D_MODEL, D_HEAD), jnp.float32) * init, 'W_V': jax.random.normal(ks[3], (N_HEADS, D_MODEL, D_HEAD), jnp.float32) * init, 'W_O': jax.random.normal(ks[4], (N_HEADS, D_HEAD, D_MODEL), jnp.float32) * init, 'b_Q': jnp.zeros((N_HEADS, D_HEAD), jnp.float32), 'b_K': jnp.zeros((N_HEADS, D_HEAD), jnp.float32), 'b_V': jnp.zeros((N_HEADS, D_HEAD), jnp.float32), 'b_O': jnp.zeros((D_MODEL,), jnp.float32)}
    _L0_attn_in = _L0_attn_setup()

    def _L0_ffn_setup():
        import jax, jax.numpy as jnp
        import numpy as np
        H = 256
        E = 8
        TOP_K = 2
        I_MOE = 176
        I_SH = 704
        BS, NT = (2, 64)
        key = jax.random.key(seed)
        ks = jax.random.split(key, 7)
        s = lambda d: (1.0 / np.sqrt(d)).astype(np.float32)
        return {'hidden_states': jax.random.normal(ks[0], (BS, NT, H), jnp.float32), 'gate_w': jax.random.normal(ks[1], (E, H), jnp.float32) * s(H), 'w1': jax.random.normal(ks[2], (E, 2 * I_MOE, H), jnp.float32) * s(H), 'w2': jax.random.normal(ks[3], (E, H, I_MOE), jnp.float32) * s(I_MOE), 'shared_gate_up_w': jax.random.normal(ks[4], (2 * I_SH, H), jnp.float32) * s(H), 'shared_down_w': jax.random.normal(ks[5], (H, I_SH), jnp.float32) * s(I_SH), 'shared_gate_w': jax.random.normal(ks[6], (1, H), jnp.float32) * s(H)}
    _L0_ffn_in = _L0_ffn_setup()
    _d = {'L0_attn_x': _L0_attn_in['x'], 'L0_attn_W_Q': _L0_attn_in['W_Q'], 'L0_attn_W_K': _L0_attn_in['W_K'], 'L0_attn_W_V': _L0_attn_in['W_V'], 'L0_attn_W_O': _L0_attn_in['W_O'], 'L0_attn_b_Q': _L0_attn_in['b_Q'], 'L0_attn_b_K': _L0_attn_in['b_K'], 'L0_attn_b_V': _L0_attn_in['b_V'], 'L0_attn_b_O': _L0_attn_in['b_O'], 'L0_ffn_gate_w': _L0_ffn_in['gate_w'], 'L0_ffn_w1': _L0_ffn_in['w1'], 'L0_ffn_w2': _L0_ffn_in['w2'], 'L0_ffn_shared_gate_up_w': _L0_ffn_in['shared_gate_up_w'], 'L0_ffn_shared_down_w': _L0_ffn_in['shared_down_w'], 'L0_ffn_shared_gate_w': _L0_ffn_in['shared_gate_w']}
    _x0 = _d['L0_attn_x']
    _d['L0_attn_x'] = jax.random.normal(jax.random.fold_in(jax.random.key(seed), 1), (4, 256, 256), dtype=_x0.dtype)
    del _x0
    return _d

def reference(L0_attn_x, L0_attn_W_Q, L0_attn_W_K, L0_attn_W_V, L0_attn_W_O, L0_attn_b_Q, L0_attn_b_K, L0_attn_b_V, L0_attn_b_O, L0_ffn_gate_w, L0_ffn_w1, L0_ffn_w2, L0_ffn_shared_gate_up_w, L0_ffn_shared_down_w, L0_ffn_shared_gate_w):

    def _L0_attn_ref(x, W_Q, W_K, W_V, W_O, b_Q, b_K, b_V, b_O):
        import jax, jax.numpy as jnp
        import numpy as np
        BATCH, SEQ, D_MODEL, N_HEADS, D_HEAD = (2, 256, 256, 16, 128)
        ATTN_SCALE = np.sqrt(D_HEAD).astype(np.float32)
        IGNORE = jnp.float32(-100000.0)
        q = jnp.einsum('bpd,hde->bphe', x, W_Q) + b_Q
        k = jnp.einsum('bpd,hde->bphe', x, W_K) + b_K
        v = jnp.einsum('bpd,hde->bphe', x, W_V) + b_V
        scores = jnp.einsum('bqhe,bkhe->bhqk', q, k) / ATTN_SCALE
        S = x.shape[1]
        causal = jnp.tril(jnp.ones((S, S), bool))
        scores = jnp.where(causal, scores, IGNORE)
        attn = jax.nn.softmax(scores, axis=-1)
        z = jnp.einsum('bkhe,bhqk->bqhe', v, attn)
        out = jnp.einsum('bqhe,hed->bqd', z, W_O) + b_O
        return out

    def _L0_ffn_ref(hidden_states, gate_w, w1, w2, shared_gate_up_w, shared_down_w, shared_gate_w):
        import jax, jax.numpy as jnp
        import numpy as np
        H = 256
        E = 8
        TOP_K = 2
        I_MOE = 176
        I_SH = 704
        BS, NT = (2, 64)
        bs, nt, h = hidden_states.shape
        x = hidden_states.reshape(-1, h)
        T = x.shape[0]
        gu = x @ shared_gate_up_w.T
        g, u = jnp.split(gu, 2, axis=-1)
        shared = jax.nn.silu(g) * u @ shared_down_w.T
        shared = jax.nn.sigmoid(x @ shared_gate_w.T) * shared
        logits = x @ gate_w.T
        probs = jax.nn.softmax(logits.astype(jnp.float32), axis=-1)
        top_w, top_i = jax.lax.top_k(probs, TOP_K)
        top_w = top_w / jnp.sum(top_w, axis=-1, keepdims=True)
        combine = jnp.zeros((T, E), top_w.dtype).at[jnp.arange(T)[:, None], top_i].set(top_w)
        gu_e = jnp.einsum('th,eih->tei', x, w1)
        ge, ue = jnp.split(gu_e, 2, axis=-1)
        he = jax.nn.silu(ge) * ue
        ye = jnp.einsum('tei,ehi->teh', he, w2)
        out = jnp.einsum('teh,te->th', ye, combine.astype(x.dtype)) + shared
        return out.reshape(bs, nt, h)
    x = L0_attn_x
    x = x + 0.5 * _L0_ffn_ref(_layernorm(x, axis=-1), L0_ffn_gate_w, L0_ffn_w1, L0_ffn_w2, L0_ffn_shared_gate_up_w, L0_ffn_shared_down_w, L0_ffn_shared_gate_w)
    x = x + _L0_attn_ref(_layernorm(x, axis=-1), L0_attn_W_Q, L0_attn_W_K, L0_attn_W_V, L0_attn_W_O, L0_attn_b_Q, L0_attn_b_K, L0_attn_b_V, L0_attn_b_O)
    x = x + 0.5 * _L0_ffn_ref(_layernorm(x, axis=-1), L0_ffn_gate_w, L0_ffn_w1, L0_ffn_w2, L0_ffn_shared_gate_up_w, L0_ffn_shared_down_w, L0_ffn_shared_gate_w)
    return x

_drawn_inputs = setup_inputs


def setup_inputs(seed=0):
    import zlib

    import numpy as np

    out = dict(_drawn_inputs(seed))
    spreads = {'L0_attn_b_Q': (0.0, 0.1),
     'L0_attn_b_K': (0.0, 0.1),
     'L0_attn_b_V': (0.0, 0.1),
     'L0_attn_b_O': (0.0, 0.1)}
    factors = {}
    for name, (base, spread) in spreads.items():
        noise = np.random.default_rng([zlib.crc32(name.encode()), seed]).standard_normal(out[name].shape)
        drawn = base * np.exp(spread * noise) if base else spread * noise
        out[name] = jnp.asarray(drawn.astype(out[name].dtype))
    for name, factor in factors.items():
        out[name] = (out[name] * factor).astype(out[name].dtype)
    return out
```

```python
import numpy as np
import concourse.bass as bass
from concourse import mybir
from contextlib import ExitStack

FP32 = mybir.dt.float32
FP32R = mybir.dt.float32r
BF16 = mybir.dt.bfloat16
I32 = mybir.dt.int32
ALU = mybir.AluOpType
ACT = mybir.ActivationFunctionType
AX = mybir.AxisListType

P = 128
BATCH, SEQ, D = 4, 256, 256
TOK = BATCH * SEQ
NT = TOK // P
KD = D // P
HALF = 512
NE = 8
TOP_K = 2
IM = 176
IC = IM // 2
ISH = 704
SC = -(-ISH // P)
ISP = SC * P
NG = NE + 2
NH, DH = 16, 128
NP = NH // 2
NM = TOP_K * NT + NE - 1
EPS = 1e-5
IGNORE = -100000.0
BIG = 3.0e38
INV_SCALE = 1.0 / float(np.sqrt(np.float32(DH)))

C_ID = 0
C_U = C_ID + P
C_ONE = C_U + P
C_MASK = C_ONE + P
C_DESC = C_MASK + 3 * P
C_M128 = C_DESC + NE
C_LT = C_M128 + NT
C_MI = C_LT + NE * NE
C_EPS = C_MI + NM
C_NH = C_EPS + NT
C_ZERO = C_NH + NT
C_N = C_ZERO + 1


def constants():
    c = np.zeros((P, C_N), np.float32)
    r = np.arange(P)
    c[:, C_ID:C_ID + P] = np.eye(P)
    c[:, C_U:C_U + P] = r[:, None] < r[None, :]
    c[:, C_ONE:C_ONE + P] = 1.0
    diagonal = np.where(r[None, :] <= r[:, None], -BIG, -IGNORE)
    c[:, C_MASK:C_MASK + P] = diagonal
    c[:, C_MASK + P:C_MASK + 2 * P] = -BIG
    c[:, C_MASK + 2 * P:C_MASK + 3 * P] = diagonal
    c[:, C_DESC:C_DESC + NE] = NE - np.arange(NE)
    c[:, C_M128:C_M128 + NT] = P * np.arange(NT)
    e = np.arange(NE)
    c[:, C_LT:C_LT + NE * NE] = (e[None, :] < e[:, None]).reshape(-1)
    c[:, C_MI:C_MI + NM] = np.arange(NM)
    c[:, C_EPS:C_EPS + NT] = EPS
    c[:, C_NH:C_NH + NT] = -0.5
    return c


def macaron(nc, x_in, consts, wgate, wgu, wd, w1, w2, wqkv, wo, bqkv, bo, out):
    ctx = ExitStack()
    with ctx:
        def sbuf(name, shape, dt=FP32, stack=ctx):
            return stack.enter_context(nc.sbuf_tensor(name, shape, dt))

        def sem(name):
            return ctx.enter_context(nc.semaphore(name))

        xg = nc.dram_tensor("x_by_expert", (NM * P, D), FP32, kind="Internal").ap()
        yg = nc.dram_tensor("y_by_expert", (NM * P, D), FP32, kind="Internal").ap()

        cst = sbuf("cst", [P, C_N])
        x_res = sbuf("x_res", [P, NT, D])
        xn = sbuf("xn", [P, NT, D])
        xT_h = sbuf("xT_h", [P, KD, TOK], FP32R)
        xT_l = sbuf("xT_l", [P, KD, TOK], FP32R)
        wg_h = sbuf("wg_h", [P, KD, NG], FP32R)
        wg_l = sbuf("wg_l", [P, KD, NG], FP32R)
        wgu_h = sbuf("wgu_h", [P, KD, 2 * ISP], FP32R)
        wgu_l = sbuf("wgu_l", [P, KD, 2 * ISP], FP32R)
        wd_h = sbuf("wd_h", [P, SC, D], FP32R)
        wd_l = sbuf("wd_l", [P, SC, D], FP32R)
        w1_h = sbuf("w1_h", [P, NE, KD, 2 * IM], FP32R)
        w1_l = sbuf("w1_l", [P, NE, KD, 2 * IM], FP32R)
        rank_w = sbuf("rank_w", [P, 2, P], BF16)
        stats = sbuf("stats", [P, NT, 6])
        mv = sbuf("mv", [P, NT, 2])
        rstd = sbuf("rstd", [P, NT])
        bank = [ctx.enter_context(nc.psum_tensor(f"bank{b}", [P, HALF], FP32)) for b in range(8)]
        ident = cst[:, C_ID:C_ID + P]
        s_gath = [sem(f"s_gath{b}") for b in range(NT)]

        def split_matmuls(pe, psum, lhs, rhs, first, last):
            pe.matmul(psum, lhs[0], rhs[0], start=first, stop=False)
            pe.matmul(psum, lhs[0], rhs[1], start=False, stop=False)
            return pe.matmul(psum, lhs[1], rhs[0], start=False, stop=last)

        def norm_stats(dve, s, tag_wait):
            for j in range(NT):
                if tag_wait is not None:
                    dve.wait_ge(tag_wait[j], 16)
                dve.bn_stats(stats[:, j, :], x_res[:, j, :]).then_inc(s["stats"], 1)
            for j in range(NT):
                dve.wait_ge(s["stats"], j + 1)
                dve.bn_aggr(mv[:, j, :], stats[:, j, :]).then_inc(s["mv"], 1)

        def norm_apply(dve, s):
            dve.wait_ge(s["rstd"], 2)
            for j in range(NT):
                dve.tensor_scalar(xn[:, j, :], x_res[:, j, :], mv[:, j, 0:1], rstd[:, j:j + 1],
                                  ALU.subtract, ALU.mult).then_inc(s["xn"], 1)

        def norm_rstd(pool, s):
            pool.wait_ge(s["mv"], NT)
            pool.tensor_tensor(rstd[:, :], mv[:, :, 1], cst[:, C_EPS:C_EPS + NT], ALU.add).then_inc(s["rstd"], 1)
            pool.wait_ge(s["rstd"], 1)
            pool.tensor_tensor(rstd[:, :], rstd[:, :], cst[:, C_NH:C_NH + NT], ALU.pow).then_inc(s["rstd"], 1)

        def norm_transposes(pe, s):
            for g in range(4):
                half, k = divmod(g, KD)
                pe.wait_ge(s["xn"], 4 * half + 4)
                for j in range(4):
                    last = pe.transpose(bank[g][:, j * P:(j + 1) * P],
                                        xn[:, 4 * half + j, k * P:(k + 1) * P], ident)
                last.then_inc(s["xt"], 1)

        def norm_split_high(act, s):
            for g in range(4):
                half, k = divmod(g, KD)
                act.wait_ge(s["xt"], g + 1)
                act.activation(xT_h[:, k, half * HALF:(half + 1) * HALF], bank[g][:, :],
                               ACT.Copy).then_inc(s["xth"], 1)

        def norm_split_low(dve, s):
            for g in range(4):
                half, k = divmod(g, KD)
                cols = slice(half * HALF, (half + 1) * HALF)
                dve.wait_ge(s["xth"], g + 1)
                dve.tensor_tensor(xT_l[:, k, cols], bank[g][:, :], xT_h[:, k, cols].bitcast(FP32),
                                  ALU.subtract).then_inc(s["xtl"], 1)

        def norm_sems(tag):
            return {n: sem(f"{n}_{tag}") for n in ("stats", "mv", "rstd", "xn", "xt", "xth", "xtl")}

        def ffn(tag, first):
            loc = ExitStack()
            with loc:
                def sb(name, shape, dt=FP32):
                    return sbuf(f"{name}_{tag}", shape, dt, loc)

                w2_h = sb("w2_h", [IC, NE, 2, D], FP32R)
                w2_l = sb("w2_l", [IC, NE, 2, D], FP32R)
                stage = [sb(f"stage{b}", [P, ISP]) for b in range(2)]
                wg_raw = sb("wg_raw", [P, KD * NG])
                hs = [sb(f"hs{b}", [P, HALF]) for b in range(2)]
                hT_h = sb("hT_h", [P, SC, HALF], FP32R)
                hT_l = sb("hT_l", [P, SC, HALF], FP32R)
                xe = [sb(f"xe{b}", [P, D]) for b in range(2)]
                xeT_h = [sb(f"xeT_h{b}", [P, KD * P], FP32R) for b in range(2)]
                xeT_l = [sb(f"xeT_l{b}", [P, KD * P], FP32R) for b in range(2)]
                he = [sb(f"he{b}", [P, IM]) for b in range(2)]
                heT_h = [sb(f"heT_h{b}", [IC, 2 * P], FP32R) for b in range(2)]
                heT_l = [sb(f"heT_l{b}", [IC, 2 * P], FP32R) for b in range(2)]
                ye = [sb(f"ye{b}", [P, D]) for b in range(2)]
                lg = sb("lg", [P, NT, NG])
                dl = sb("dl", [P, NT, NE])
                sc = sb("sc", [P, NT, NE])
                sel = [sb(f"sel{b}", [P, NT, NE]) for b in range(TOP_K)]
                assigned = sb("assigned", [P, NT * NE], BF16)
                best = sb("best", [P, NT])
                best2 = sb("best2", [P, NT])
                lead = sb("lead", [P, NT])
                rank = sb("rank", [P, 2, NT, NE])
                cum = sb("cum", [P, NT + 1, NE])
                cmp = sb("cmp", [P, NE, NE])
                tiles_of = sb("tiles_of", [P, NE])
                base = sb("base", [P, NE])
                end = sb("end", [P, NE])
                slot = sb("slot", [P, NT, NE])
                slot_f = sb("slot_f", [P, TOP_K, NT])
                slot_i = sb("slot_i", [P, TOP_K * NT], I32)
                tile_cmp = sb("tile_cmp", [1, NM, NE])
                tile_f = sb("tile_f", [1, NM])
                tile_e = sb("tile_e", [1, NM], I32)
                gates = sb("gates", [P, 2, NT])
                gates_r = sb("gates_r", [P, 2, NT])
                cw2 = sb("cw2", [P, NT])

                n = norm_sems(tag)
                s_x = [sem(f"s_x{j}_{tag}") for j in range(NT)] if first else None
                s_cst = sem(f"s_cst_{tag}")
                s_rw = sem(f"s_rw_{tag}")
                s_stage = [sem(f"s_stage{b}_{tag}") for b in range(2)]
                s_wh = sem(f"s_wh_{tag}")
                s_wl = sem(f"s_wl_{tag}")
                s_gate_in = sem(f"s_gate_in_{tag}")
                s_gh = sem(f"s_gh_{tag}")
                s_gl = sem(f"s_gl_{tag}")
                s_logits = sem(f"s_logits_{tag}")
                s_route = sem(f"s_route_{tag}")
                s_exp = sem(f"s_exp_{tag}")
                s_assigned = sem(f"s_assigned_{tag}")
                s_rank = sem(f"s_rank_{tag}")
                s_rank_sb = sem(f"s_rank_sb_{tag}")
                s_slot = sem(f"s_slot_{tag}")
                s_expert = sem(f"s_expert_{tag}")
                s_zero = sem(f"s_zero_{tag}")
                s_zfill = sem(f"s_zfill_{tag}")
                s_scat = sem(f"s_scat_{tag}")
                s_up = sem(f"s_up_{tag}")
                s_silu = sem(f"s_silu_{tag}")
                s_hm = sem(f"s_hm_{tag}")
                s_hh = sem(f"s_hh_{tag}")
                s_hl = sem(f"s_hl_{tag}")
                s_dn = sem(f"s_dn_{tag}")
                s_dnv = sem(f"s_dnv_{tag}")
                s_xe = [sem(f"s_xe{b}_{tag}") for b in range(2)]
                s_tx = sem(f"s_tx_{tag}")
                s_txh = sem(f"s_txh_{tag}")
                s_txl = sem(f"s_txl_{tag}")
                s_eu = sem(f"s_eu_{tag}")
                s_es = sem(f"s_es_{tag}")
                s_em = sem(f"s_em_{tag}")
                s_th = sem(f"s_th_{tag}")
                s_thh = sem(f"s_thh_{tag}")
                s_thl = sem(f"s_thl_{tag}")
                s_ed = sem(f"s_ed_{tag}")
                s_ye = sem(f"s_ye_{tag}")
                s_yst = [sem(f"s_yst{b}_{tag}") for b in range(2)]
                s_add = sem(f"s_add_{tag}")
                s_out = sem(f"s_out_{tag}")

                jobs = []
                if first:
                    for g in range(2):
                        for k in range(KD):
                            cols = slice(g * ISP, (g + 1) * ISP)
                            jobs.append((wgu[:, k, cols], wgu_h[:, k, cols], wgu_l[:, k, cols]))
                    for a in range(0, SC, 3):
                        jobs.append((wd[:, a:a + 3, :], wd_h[:, a:a + 3, :], wd_l[:, a:a + 3, :]))
                    early = len(jobs)
                    for e in range(NE):
                        jobs.append((w1[:, e], w1_h[:, e], w1_l[:, e]))
                else:
                    early = 0
                for e in range(NE):
                    jobs.append((w2[:, e], w2_h[:, e], w2_l[:, e]))
                before_up = min(4, early)

                def flat(ap):
                    return ap.rearrange("p a b -> p (a b)") if len(ap.shape) == 3 else ap

                def job_high(act, q):
                    src, high, _ = jobs[q]
                    act.wait_ge(s_stage[q % 2], 16 * (q // 2 + 1))
                    rows, cols = flat(high).shape
                    act.activation(flat(high), stage[q % 2][0:rows, 0:cols], ACT.Copy).then_inc(s_wh, 1)

                def job_low(dve, q):
                    _, high, low = jobs[q]
                    dve.wait_ge(s_wh, q + 1)
                    rows, cols = flat(high).shape
                    dve.tensor_tensor(flat(low), stage[q % 2][0:rows, 0:cols], flat(high).bitcast(FP32),
                                      ALU.subtract).then_inc(s_wl, 1)

                late = list(range(early, len(jobs)))
                share = -(-len(late) // SC)
                late_of = [late[c * share:(c + 1) * share] for c in range(SC)]

                block_ctx = ExitStack()
                block = block_ctx.enter_context(nc.Block())

                @block.sync
                def _(sp):
                    if first:
                        xv = x_in.rearrange("(j p) d -> p j d", p=P)
                        sp.dma_start(x_res[:, 0, :], xv[:, 0, :]).then_inc(s_x[0], 16)
                        sp.dma_start(cst[:, :], consts).then_inc(s_cst, 16)
                        for j in range(1, NT):
                            sp.dma_start(x_res[:, j, :], xv[:, j, :]).then_inc(s_x[j], 16)
                        sp.dma_start(wg_raw[:, :], wgate).then_inc(s_gate_in, 16)
                    for q, (src, high, _) in enumerate(jobs):
                        if q >= 2:
                            sp.wait_ge(s_wl, q - 1)
                        rows, cols = flat(high).shape
                        sp.dma_start(stage[q % 2][0:rows, 0:cols], flat(src)).then_inc(s_stage[q % 2], 16)
                        if first and q == 1:
                            sp.wait_ge(s_zero, 1)
                            sp.dma_start(xg.rearrange("(m p) d -> p m d", p=P),
                                         hs[0][:, 0:D].unsqueeze(1).to_broadcast([P, NM, D])).then_inc(s_zfill, 16)

                    def load(m, q, b):
                        sp.dma_start(xe[b][:, :], xg[bass.ds(m * P, P), :]).then_inc(s_xe[b], 16)

                    sp.wait_ge(s_scat, 16 * TOP_K * NT)
                    load(0, 0, 0)
                    load(1, 0, 1)
                    with sp.Fori(0, (NM - 3) // 2) as i:
                        for b in range(2):
                            sp.wait_ge(s_tx, 2 * i + b + 1)
                            load(2 * i + 2 + b, i + 1, b)
                    sp.wait_ge(s_tx, NM - 2)
                    load(NM - 1, (NM - 1) // 2, 0)
                    if not first:
                        ov = out.rearrange("(j p) d -> p j d", p=P)
                        for j in range(NT):
                            sp.wait_ge(s_add, TOP_K * (j + 1))
                            sp.wait_ge(s_dnv, j + 1)
                            sp.dma_start(ov[:, j, :], x_res[:, j, :]).then_inc(s_out, 16)
                        sp.wait_ge(s_out, 16 * NT)

                @block.gpsimd
                def _(pool):
                    if first:
                        pool.memset(hs[0][:, 0:D], 0.0).then_inc(s_zero, 1)
                        pool.wait_ge(s_cst, 16)
                    norm_rstd(pool, n)
                    pool.wait_ge(n["xn"], NT)
                    pool.wait_ge(s_slot, 1)
                    if first:
                        pool.wait_ge(s_zfill, 16)
                    for j in range(NT):
                        for t in range(TOP_K):
                            col = t * NT + j
                            pool.indirect_dma_start(
                                xg, bass.IndirectOffsetOnAxis(ap=slot_i[:, col:col + 1], axis=0),
                                xn[:, j, :], None).then_inc(s_scat, 16)

                    def store(m, b):
                        pool.wait_ge(s_ye, m + 1)
                        pool.dma_start(yg[bass.ds(m * P, P), :], ye[b][:, :]).then_inc(s_yst[b], 16)

                    with pool.Fori(0, (NM - 1) // 2) as i:
                        for b in range(2):
                            store(2 * i + b, b)
                    store(NM - 1, 0)
                    pool.wait_ge(s_yst[0], 16 * ((NM + 1) // 2))
                    pool.wait_ge(s_yst[1], 16 * (NM // 2))
                    pool.wait_ge(s_scat, 16 * TOP_K * NT)
                    for g in range(TOP_K * NT):
                        j, t = divmod(g, TOP_K)
                        if g >= NT:
                            pool.wait_ge(s_add, g - NT + 1)
                        col = t * NT + j
                        pool.indirect_dma_start(
                            xn[:, g % NT, :], None, yg,
                            bass.IndirectOffsetOnAxis(ap=slot_i[:, col:col + 1], axis=0)).then_inc(s_gath[g % NT], 16)

                @block.scalar
                def _(act):
                    if first:
                        for q in range(before_up):
                            job_high(act, q)
                        act.wait_ge(s_gate_in, 16)
                        act.activation(flat(wg_h[:, :, :]), wg_raw[:, :], ACT.Copy).then_inc(s_gh, 1)
                    norm_split_high(act, n)
                    act.wait_ge(s_route, 8)
                    act.activation(gates[:, 0, :], best2[:, :], ACT.Exp).then_inc(s_exp, 1)
                    act.activation(gates[:, 1, :], lg[:, :, NE], ACT.Exp, scale=-1.0).then_inc(s_exp, 1)

                    def shared_silu(c):
                        act.wait_ge(s_up, c + 1)
                        if c >= 2:
                            act.wait_ge(s_hl, c - 1)
                        act.activation(hs[c % 2][:, :], bank[2 * (c % 2)][:, :], ACT.Silu).then_inc(s_silu, 1)

                    def shared_high(c):
                        act.wait_ge(s_hm, c + 1)
                        act.activation(hT_h[:, c % SC, :], hs[c % 2][:, :], ACT.Copy).then_inc(s_hh, 1)

                    for c in range(SC):
                        if first and c == 0:
                            act.wait_ge(s_zfill, 16)
                        shared_silu(c)
                        if c == 0:
                            for q in range(before_up, early):
                                job_high(act, q)
                        if c == 1:
                            act.wait_ge(s_rank, 1)
                            act.activation(rank[:, :, :, :].rearrange("p a b c -> p (a b c)"),
                                           bank[5][:, 0:2 * NT * NE], ACT.Copy).then_inc(s_rank_sb, 1)
                        for q in late_of[c]:
                            job_high(act, q)
                        shared_high(c)

                    def tile_high(m, b):
                        act.wait_ge(s_tx, m + 1)
                        act.activation(xeT_h[b][:, :], bank[b][:, 0:KD * P], ACT.Copy).then_inc(s_txh, 1)

                    def inner_high(m, b):
                        act.wait_ge(s_th, m + 1)
                        act.activation(heT_h[b][:, :], bank[4 + b][0:IC, 0:2 * P], ACT.Copy).then_inc(s_thh, 1)

                    def inner_silu(m, b):
                        act.wait_ge(s_eu, m + 1)
                        act.activation(he[b][:, :], bank[2 + b][:, 0:IM], ACT.Silu).then_inc(s_es, 1)

                    def tile_out(m, q, b, guard=True):
                        act.wait_ge(s_ed, m + 1)
                        if guard:
                            act.wait_ge(s_yst[b], 16 * q)
                        act.activation(ye[b][:, :], bank[6 + b][:, 0:D], ACT.Copy).then_inc(s_ye, 1)

                    tile_high(0, 0)
                    inner_silu(0, 0)
                    tile_high(1, 1)
                    inner_high(0, 0)
                    inner_silu(1, 1)
                    tile_high(2, 0)
                    tile_out(0, 0, 0, False)
                    inner_high(1, 1)
                    inner_silu(2, 0)
                    tile_high(3, 1)
                    tile_out(1, 0, 1, False)
                    with act.Fori(1, (NM - 3) // 2) as i:
                        inner_high(2 * i, 0)
                        inner_silu(2 * i + 1, 1)
                        tile_high(2 * i + 2, 0)
                        tile_out(2 * i, i, 0)
                        inner_high(2 * i + 1, 1)
                        inner_silu(2 * i + 2, 0)
                        tile_high(2 * i + 3, 1)
                        tile_out(2 * i + 1, i, 1)
                    m = NM - 2
                    inner_high(m - 1, 0)
                    inner_silu(m, 1)
                    tile_high(m + 1, 0)
                    tile_out(m - 1, (m - 1) // 2, 0)
                    inner_high(m, 1)
                    inner_silu(m + 1, 0)
                    tile_out(m, m // 2, 1)
                    inner_high(m + 1, 0)
                    tile_out(m + 1, (m + 1) // 2, 0)
                    for c in range(SC, 2 * SC):
                        shared_silu(c)
                        shared_high(c)

                @block.vector
                def _(dve):
                    steps = [0]

                    def link(ins):
                        steps[0] += 1
                        ins.then_inc(s_route, 1)
                        dve.wait_ge(s_route, steps[0])

                    norm_stats(dve, n, s_x)
                    for q in range(before_up):
                        job_low(dve, q)
                    norm_apply(dve, n)
                    if first:
                        dve.wait_ge(s_gh, 1)
                        dve.tensor_tensor(flat(wg_l[:, :, :]), wg_raw[:, :], flat(wg_h[:, :, :]).bitcast(FP32),
                                          ALU.subtract).then_inc(s_gl, 1)
                        dve.tensor_copy(rank_w[:, :, :].rearrange("p a b -> p (a b)"),
                                        cst[:, C_U:C_ONE + P]).then_inc(s_rw, 1)
                    norm_split_low(dve, n)

                    def wide(ap):
                        return ap.unsqueeze(2).to_broadcast([P, NT, NE])

                    desc = cst[:, C_DESC:C_DESC + NE].unsqueeze(1).to_broadcast([P, NT, NE])
                    dve.wait_ge(s_logits, 1)
                    link(dve.tensor_copy(flat(lg[:, :, :]), bank[4][:, 0:NT * NG]))
                    link(dve.tensor_reduce(best[:, :], lg[:, :, 0:NE], op=ALU.max, axis=AX.X))
                    link(dve.tensor_tensor(dl[:, :, :], lg[:, :, 0:NE], wide(best[:, :]), ALU.subtract))
                    link(dve.scalar_tensor_tensor(sc[:, :, :], dl[:, :, :], 0.0, desc, ALU.is_ge, ALU.mult))
                    link(dve.tensor_reduce(lead[:, :], sc[:, :, :], op=ALU.max, axis=AX.X))
                    link(dve.tensor_tensor(sel[0][:, :, :], sc[:, :, :], wide(lead[:, :]), ALU.is_equal))
                    link(dve.scalar_tensor_tensor(dl[:, :, :], sel[0][:, :, :], -BIG, dl[:, :, :], ALU.mult, ALU.add))
                    link(dve.tensor_reduce(best2[:, :], dl[:, :, :], op=ALU.max, axis=AX.X))
                    link(dve.tensor_tensor(dl[:, :, :], dl[:, :, :], wide(best2[:, :]), ALU.is_equal))
                    link(dve.tensor_tensor(sc[:, :, :], dl[:, :, :], desc, ALU.mult))
                    link(dve.tensor_reduce(lead[:, :], sc[:, :, :], op=ALU.max, axis=AX.X))
                    link(dve.tensor_tensor(sel[1][:, :, :], sc[:, :, :], wide(lead[:, :]), ALU.is_equal))
                    dve.tensor_tensor(assigned[:, :], flat(sel[0][:, :, :]), flat(sel[1][:, :, :]),
                                      ALU.add).then_inc(s_assigned, 1)

                    def shared_mul(c):
                        dve.wait_ge(s_silu, c + 1)
                        dve.tensor_tensor(hs[c % 2][:, :], hs[c % 2][:, :], bank[2 * (c % 2) + 1][:, :],
                                          ALU.mult).then_inc(s_hm, 1)

                    def shared_low(c):
                        dve.wait_ge(s_hh, c + 1)
                        dve.tensor_tensor(hT_l[:, c % SC, :], hs[c % 2][:, :], hT_h[:, c % SC, :].bitcast(FP32),
                                          ALU.subtract).then_inc(s_hl, 1)

                    def shared_out(j):
                        dve.wait_ge(s_dn, j + 1)
                        dve.scalar_tensor_tensor(x_res[:, j, :], bank[6 + j % 2][:, 0:D], gates_r[:, 1, j:j + 1],
                                                 x_res[:, j, :], ALU.mult, ALU.add).then_inc(s_dnv, 1)

                    def slots():
                        link(dve.memset(cum[:, 0, :], 0.0))
                        dve.wait_ge(s_rank_sb, 1)
                        for j in range(NT):
                            link(dve.tensor_tensor(cum[:, j + 1, :], cum[:, j, :], rank[:, 1, j, :], ALU.add))
                        link(dve.tensor_tensor(cmp[:, :, :], wide(cum[:, NT, :]),
                                               cst[:, C_M128:C_M128 + NT].unsqueeze(1).to_broadcast([P, NE, NT]),
                                               ALU.is_gt))
                        link(dve.tensor_reduce(tiles_of[:, :], cmp[:, :, :], op=ALU.add, axis=AX.X))
                        link(dve.tensor_tensor(cmp[:, :, :], tiles_of[:, :].unsqueeze(1).to_broadcast([P, NE, NE]),
                                               cst[:, C_LT:C_LT + NE * NE].rearrange("p (a b) -> p a b", a=NE),
                                               ALU.mult))
                        link(dve.tensor_reduce(base[:, :], cmp[:, :, :], op=ALU.add, axis=AX.X))
                        link(dve.tensor_tensor(slot[:, :, :], rank[:, 0], cum[:, 0:NT, :], ALU.add))
                        link(dve.scalar_tensor_tensor(slot[:, :, :],
                                                      base[:, :].unsqueeze(1).to_broadcast([P, NT, NE]), float(P),
                                                      slot[:, :, :], ALU.mult, ALU.add))
                        for t in range(TOP_K):
                            link(dve.tensor_tensor(sel[t][:, :, :], sel[t][:, :, :], slot[:, :, :], ALU.mult))
                            link(dve.tensor_reduce(slot_f[:, t, :], sel[t][:, :, :], op=ALU.add, axis=AX.X))
                        dve.tensor_copy(slot_i[:, :], flat(slot_f[:, :, :])).then_inc(s_slot, 1)
                        link(dve.tensor_tensor(end[:, :], base[:, :], tiles_of[:, :], ALU.add))
                        link(dve.tensor_tensor(tile_cmp[0:1, :, :],
                                               cst[0:1, C_MI:C_MI + NM].unsqueeze(2).to_broadcast([1, NM, NE]),
                                               end[0:1, :].unsqueeze(1).to_broadcast([1, NM, NE]), ALU.is_ge))
                        link(dve.tensor_reduce(tile_f[0:1, :], tile_cmp[0:1, :, :], op=ALU.add, axis=AX.X))
                        dve.tensor_scalar(tile_e[0:1, :], tile_f[0:1, :], float(NE - 1), None,
                                          ALU.min).then_inc(s_expert, 1)

                    def weights():
                        dve.wait_ge(s_exp, 2)
                        link(dve.tensor_scalar(gates_r[:, :, :], gates[:, :, :], 1.0, None, ALU.add))
                        link(dve.reciprocal(gates_r[:, :, :], gates_r[:, :, :]))
                        link(dve.tensor_scalar(gates_r[:, :, :], gates_r[:, :, :], 0.5, None, ALU.mult))
                        link(dve.tensor_tensor(cw2[:, :], gates[:, 0, :], gates_r[:, 0, :], ALU.mult))

                    for c in range(SC):
                        shared_mul(c)
                        if c == 0:
                            for q in range(before_up, early):
                                job_low(dve, q)
                        if c == 1:
                            slots()
                            weights()
                        for q in late_of[c]:
                            job_low(dve, q)
                        shared_low(c)
                    for j in range(NT // 2):
                        shared_out(j)

                    def tile_low(m, b):
                        dve.wait_ge(s_txh, m + 1)
                        dve.tensor_tensor(xeT_l[b][:, :], bank[b][:, 0:KD * P], xeT_h[b][:, :].bitcast(FP32),
                                          ALU.subtract).then_inc(s_txl, 1)

                    def inner_low(m, b):
                        dve.wait_ge(s_thh, m + 1)
                        dve.tensor_tensor(heT_l[b][:, :], bank[4 + b][0:IC, 0:2 * P], heT_h[b][:, :].bitcast(FP32),
                                          ALU.subtract).then_inc(s_thl, 1)

                    def inner_mul(m, b):
                        dve.wait_ge(s_es, m + 1)
                        dve.tensor_tensor(he[b][:, :], he[b][:, :], bank[2 + b][:, IM:2 * IM],
                                          ALU.mult).then_inc(s_em, 1)

                    tile_low(0, 0)
                    inner_mul(0, 0)
                    tile_low(1, 1)
                    with dve.Fori(0, (NM - 3) // 2) as i:
                        inner_low(2 * i, 0)
                        inner_mul(2 * i + 1, 1)
                        tile_low(2 * i + 2, 0)
                        inner_low(2 * i + 1, 1)
                        inner_mul(2 * i + 2, 0)
                        tile_low(2 * i + 3, 1)
                    m = NM - 2
                    inner_low(m - 1, 0)
                    inner_mul(m, 1)
                    tile_low(m + 1, 0)
                    inner_low(m, 1)
                    inner_mul(m + 1, 0)
                    inner_low(m + 1, 0)

                    def add(g):
                        j, t = divmod(g, TOP_K)
                        dve.wait_ge(s_gath[g % NT], 16 * (g // NT + 1 + (0 if first else TOP_K)))
                        if g:
                            dve.wait_ge(s_add, g)
                        w = gates_r[:, 0, j:j + 1] if t == 0 else cw2[:, j:j + 1]
                        dve.scalar_tensor_tensor(x_res[:, j, :], xn[:, g % NT, :], w, x_res[:, j, :],
                                                 ALU.mult, ALU.add).then_inc(s_add, 1)

                    dve.wait_ge(s_dnv, NT // 2)
                    g = 0
                    for c in range(SC, 2 * SC):
                        shared_mul(c)
                        shared_low(c)
                        for _ in range(2 if c >= SC + 2 else 0):
                            add(g)
                            g += 1
                    for j in range(NT // 2, NT):
                        shared_out(j)
                    dve.wait_ge(s_dnv, NT)
                    while g < TOP_K * NT:
                        add(g)
                        g += 1

                @block.tensor
                def _(pe):
                    if first:
                        pe.wait_ge(s_cst, 16)
                    norm_transposes(pe, n)
                    pe.wait_ge(n["xth"], 4)
                    pe.wait_ge(n["xtl"], 4)
                    if first:
                        pe.wait_ge(s_gh, 1)
                        pe.wait_ge(s_gl, 1)
                    for j in range(NT):
                        toks = slice(j * P, (j + 1) * P)
                        for k in range(KD):
                            last = split_matmuls(pe, bank[4][:, j * NG:(j + 1) * NG],
                                                 (xT_h[:, k, toks], xT_l[:, k, toks]),
                                                 (wg_h[:, k, :], wg_l[:, k, :]), k == 0, k == KD - 1)
                    last.then_inc(s_logits, 1)
                    if first:
                        pe.wait_ge(s_wh, 4)
                        pe.wait_ge(s_wl, 4)

                    def shared_up(c):
                        half, ch = divmod(c, SC)
                        if c >= 2:
                            pe.wait_ge(s_hm, c - 1)
                        toks = slice(half * HALF, (half + 1) * HALF)
                        for g in range(2):
                            cols = slice(g * ISP + ch * P, g * ISP + (ch + 1) * P)
                            for k in range(KD):
                                last = split_matmuls(pe, bank[2 * (c % 2) + g][:, :],
                                                     (wgu_h[:, k, cols], wgu_l[:, k, cols]),
                                                     (xT_h[:, k, toks], xT_l[:, k, toks]), k == 0, k == KD - 1)
                        last.then_inc(s_up, 1)

                    def shared_down(half):
                        pe.wait_ge(s_hh, SC * (half + 1))
                        pe.wait_ge(s_hl, SC * (half + 1))
                        for j in range(4 * half, 4 * half + 4):
                            if j % 4 >= 2:
                                pe.wait_ge(s_dnv, j - 1)
                            toks = slice((j % 4) * P, (j % 4 + 1) * P)
                            for c in range(SC):
                                last = split_matmuls(pe, bank[6 + j % 2][:, 0:D],
                                                     (hT_h[:, c, toks], hT_l[:, c, toks]),
                                                     (wd_h[:, c, :], wd_l[:, c, :]), c == 0, c == SC - 1)
                            last.then_inc(s_dn, 1)

                    shared_up(0)
                    shared_up(1)
                    if first:
                        pe.wait_ge(s_rw, 1)
                    pe.wait_ge(s_assigned, 1)
                    for a in range(2):
                        last = pe.matmul(bank[5][:, a * NT * NE:(a + 1) * NT * NE], rank_w[:, a, :], assigned[:, :],
                                         start=True, stop=True)
                    last.then_inc(s_rank, 1)
                    for c in range(2, SC):
                        shared_up(c)
                    if first:
                        pe.wait_ge(s_wl, early)
                    shared_down(0)

                    def tile_in(m, q, b):
                        pe.wait_ge(s_xe[b], 16 * (q + 1))
                        for k in range(KD):
                            last = pe.transpose(bank[b][:, k * P:(k + 1) * P], xe[b][:, k * P:(k + 1) * P], ident)
                        last.then_inc(s_tx, 1)

                    def expert_of(m):
                        return pe.value_load(tile_e[0:1, bass.ds(m, 1)], min_val=0, max_val=NE - 1)

                    def up(m, b):
                        e = expert_of(m)
                        pe.wait_ge(s_txh, m + 1)
                        pe.wait_ge(s_txl, m + 1)
                        for k in range(KD):
                            part = slice(k * P, (k + 1) * P)
                            last = split_matmuls(pe, bank[2 + b][:, 0:2 * IM],
                                                 (xeT_h[b][:, part], xeT_l[b][:, part]),
                                                 (w1_h[:, e, k, :], w1_l[:, e, k, :]), k == 0, k == KD - 1)
                        last.then_inc(s_eu, 1)

                    def inner_turn(m, b):
                        pe.wait_ge(s_em, m + 1)
                        for c in range(2):
                            last = pe.transpose(bank[4 + b][0:IC, c * P:(c + 1) * P],
                                                he[b][:, c * IC:(c + 1) * IC], ident)
                        last.then_inc(s_th, 1)

                    def down(m, b, guard=True):
                        e = expert_of(m)
                        pe.wait_ge(s_thh, m + 1)
                        pe.wait_ge(s_thl, m + 1)
                        if guard:
                            pe.wait_ge(s_ye, m - 1)
                        for c in range(2):
                            part = slice(c * P, (c + 1) * P)
                            last = split_matmuls(pe, bank[6 + b][:, 0:D],
                                                 (heT_h[b][:, part], heT_l[b][:, part]),
                                                 (w2_h[:, e, c, :], w2_l[:, e, c, :]), c == 0, c == 1)
                        last.then_inc(s_ed, 1)

                    tile_in(0, 0, 0)
                    pe.wait_ge(s_wh, len(jobs))
                    pe.wait_ge(s_wl, len(jobs))
                    pe.wait_ge(s_expert, 1)
                    pe.wait_ge(s_dnv, NT // 2)
                    up(0, 0)
                    tile_in(1, 0, 1)
                    inner_turn(0, 0)
                    up(1, 1)
                    tile_in(2, 1, 0)
                    down(0, 0, False)
                    inner_turn(1, 1)
                    up(2, 0)
                    tile_in(3, 1, 1)
                    down(1, 1, False)
                    with pe.Fori(1, (NM - 3) // 2) as i:
                        inner_turn(2 * i, 0)
                        up(2 * i + 1, 1)
                        tile_in(2 * i + 2, i + 1, 0)
                        down(2 * i, 0)
                        inner_turn(2 * i + 1, 1)
                        up(2 * i + 2, 0)
                        tile_in(2 * i + 3, i + 1, 1)
                        down(2 * i + 1, 1)
                    m = NM - 2
                    inner_turn(m - 1, 0)
                    up(m, 1)
                    tile_in(m + 1, (m + 1) // 2, 0)
                    down(m - 1, 0)
                    inner_turn(m, 1)
                    up(m + 1, 0)
                    down(m, 1)
                    inner_turn(m + 1, 0)
                    down(m + 1, 0)
                    for c in range(SC, 2 * SC):
                        shared_up(c)
                    pe.wait_ge(s_ye, NM)
                    shared_down(1)

                block_ctx.close()

        def attention():
            loc = ExitStack()
            with loc:
                def sb(name, shape, dt=FP32):
                    return sbuf(f"{name}_a", shape, dt, loc)

                QKV = 3 * KD * 2 * DH
                w_raw = sb("w_raw", [P, QKV])
                w_h = sb("w_h", [P, 3, KD, 2 * DH], FP32R)
                w_l = sb("w_l", [P, 3, KD, 2 * DH], FP32R)
                wo_raw = sb("wo_raw", [P, 2 * D])
                wo_h = sb("wo_h", [P, 2, D], FP32R)
                wo_l = sb("wo_l", [P, 2, D], FP32R)
                qk = sb("qk", [P, 2, 2, TOK])
                v = sb("v", [P, NT, 2 * DH])
                bias_all = sb("bias_all", [P, 3, NH])
                bias = sb("bias", [P, 3, 2])
                bo_sb = sb("bo_sb", [P, D])
                NS = 4
                s = [sb(f"s{b}", [P, 3 * P]) for b in range(NS)]
                mn = sb("mn", [P, NS, 2])
                rs = sb("rs", [P, NS, 2])
                rr = sb("rr", [P, NS, 2])
                pT = [sb(f"pT{b}", [P, 3 * P]) for b in range(2)]
                zT_h = sb("zT_h", [P, 2, TOK], FP32R)
                zT_l = sb("zT_l", [P, 2, TOK], FP32R)

                n = norm_sems("a")
                s_b = sem("a_bias")
                s_bo = sem("a_bo")
                s_bp = sem("a_bias_pair")
                s_wraw = sem("a_wraw")
                s_woraw = sem("a_woraw")
                s_wh = sem("a_wh")
                s_wl = sem("a_wl")
                s_woh = sem("a_woh")
                s_wol = sem("a_wol")
                s_proj = sem("a_proj")
                s_pa = sem("a_proj_act")
                s_pv = sem("a_proj_dve")
                s_sc = sem("a_scores")
                s_sm = sem("a_masked")
                s_mn = sem("a_min")
                s_e = sem("a_exp")
                s_rr = sem("a_recip")
                s_p = sem("a_probs")
                s_pt = sem("a_pT_psum")
                s_ptv = sem("a_pT")
                s_z = sem("a_z_psum")
                s_zh = sem("a_zh")
                s_zl = sem("a_zl")
                s_o = sem("a_o_psum")
                s_ov = sem("a_o_added")
                U = 2 * BATCH
                PROJ = 12
                RING = 3

                def unit(u):
                    return u // 2, u % 2

                block_ctx = ExitStack()
                block = block_ctx.enter_context(nc.Block())

                @block.sync
                def _(sp):
                    sp.dma_start(w_raw[:, :], wqkv[0]).then_inc(s_wraw, 16)
                    sp.dma_start(wo_raw[:, :], wo[0]).then_inc(s_woraw, 16)
                    sp.dma_start(bias_all[:, :, :], bqkv).then_inc(s_b, 16)
                    sp.dma_start(bo_sb[:, :], bo.partition_broadcast(P)).then_inc(s_bo, 16)
                    with sp.Fori(1, NP) as i:
                        sp.wait_ge(s_wl, i)
                        sp.dma_start(w_raw[:, :], wqkv[i]).then_inc(s_wraw, 16)
                        sp.wait_ge(s_wol, i)
                        sp.dma_start(wo_raw[:, :], wo[i]).then_inc(s_woraw, 16)

                PIECE = QKV // 6
                zero = cst[:, C_ZERO:C_ZERO + 1]

                @block.gpsimd
                def _(pool):
                    def w_flat(t):
                        return t[:, :, :, :].rearrange("p a b c -> p (a b c)")

                    def o_flat(t):
                        return t[:, :, :].rearrange("p a b -> p (a b)")

                    def split_qkv(i, c):
                        if c == 0:
                            pool.wait_ge(s_wraw, 16 * (i + 1))
                        cols = slice(c * PIECE, (c + 1) * PIECE)
                        pool.tensor_tensor(w_flat(w_h)[:, cols], w_raw[:, cols], zero.to_broadcast([P, PIECE]),
                                           ALU.add).then_inc(s_wh, 1)
                        pool.wait_ge(s_wh, 6 * i + c + 1)
                        ins = pool.tensor_tensor(w_flat(w_l)[:, cols], w_raw[:, cols],
                                                 w_flat(w_h)[:, cols].bitcast(FP32), ALU.subtract)
                        if c == 5:
                            ins.then_inc(s_wl, 1)

                    norm_rstd(pool, n)
                    for c in range(6):
                        split_qkv(0, c)

                    def body(i, more):
                        pool.wait_ge(s_woraw, 16 * (i + 1))
                        if more != "first":
                            pool.wait_ge(s_o, BATCH * i)
                        pool.tensor_tensor(o_flat(wo_h), wo_raw[:, :], zero.to_broadcast([P, 2 * D]),
                                           ALU.add).then_inc(s_woh, 1)
                        pool.wait_ge(s_woh, i + 1)
                        pool.tensor_tensor(o_flat(wo_l), wo_raw[:, :], o_flat(wo_h).bitcast(FP32),
                                           ALU.subtract).then_inc(s_wol, 1)
                        for u in range(U):
                            pool.wait_ge(s_rr, U * i + u + 1)
                            b = u % NS
                            pool.tensor_tensor(s[b][:, 0:P], s[b][:, 0:P],
                                               rr[:, b, 0:1].to_broadcast([P, P]), ALU.mult).then_inc(s_p, 1)
                            pool.tensor_tensor(s[b][:, P:3 * P], s[b][:, P:3 * P],
                                               rr[:, b, 1:2].to_broadcast([P, 2 * P]), ALU.mult).then_inc(s_p, 1)
                            if more != "last" and u < 6:
                                split_qkv(i + 1, u)

                    body(0, "first")
                    with pool.Fori(1, NP - 1) as i:
                        body(i, "more")
                    body(NP - 1, "last")

                def proj_out(g, t):
                    if g < 8:
                        return qk[:, g // 4, (g // 2) % 2, (g % 2) * HALF:(g % 2 + 1) * HALF]
                    return v[:, 2 * (g - 8):2 * (g - 8) + 2, :].rearrange("p a b -> p (a b)")

                @block.scalar
                def _(act):
                    norm_split_high(act, n)

                    def proj(i, g):
                        act.wait_ge(s_proj, PROJ * i + g + 1)
                        b = (g) % RING
                        if g < 8:
                            act.activation(proj_out(g, None), bank[b][:, :], ACT.Identity,
                                           bias=bias[:, g // 4, (g // 2) % 2:(g // 2) % 2 + 1]).then_inc(s_pa, 1)
                        else:
                            act.activation(proj_out(g, None), bank[b][:, :], ACT.Copy).then_inc(s_pa, 1)

                    def exps(i, u):
                        b = u % NS
                        act.wait_ge(s_mn, 2 * (U * i + u + 1))
                        for t, cols in ((0, slice(0, P)), (1, slice(P, 3 * P))):
                            act.activation(s[b][:, cols], s[b][:, cols], ACT.Exp, bias=mn[:, b, t:t + 1], scale=-1.0,
                                           accum_out=rs[:, b, t:t + 1]).then_inc(s_e, 1)

                    def turned(i, u):
                        act.wait_ge(s_pt, U * i + u + 1)
                        act.activation(pT[u % 2][:, :], bank[5 + u % 2][:, 0:3 * P], ACT.Copy).then_inc(s_ptv, 1)

                    def z_high(i, u):
                        bt, h = unit(u)
                        act.wait_ge(s_z, U * i + u + 1)
                        act.activation(zT_h[:, h, bt * SEQ:(bt + 1) * SEQ], bank[7][:, 0:SEQ], ACT.Identity,
                                       bias=bias[:, 2, h:h + 1]).then_inc(s_zh, 1)

                    with act.Fori(0, NP) as i:
                        act.wait_ge(s_bp, i + 1)
                        for g in range(0, PROJ, 2):
                            proj(i, g)
                        exps(i, 0)
                        exps(i, 1)
                        for u in range(U):
                            turned(i, u)
                            if u + 2 < U:
                                exps(i, u + 2)
                            z_high(i, u)

                @block.vector
                def _(dve):
                    norm_stats(dve, n, None)
                    norm_apply(dve, n)
                    norm_split_low(dve, n)
                    dve.wait_ge(s_b, 16)
                    dve.wait_ge(s_bo, 16)
                    dve.wait_ge(n["xn"], NT)
                    for j in range(NT):
                        last = dve.tensor_tensor(x_res[:, j, :], x_res[:, j, :], bo_sb[:, :], ALU.add)
                    last.then_inc(s_bo, 1)
                    dve.tensor_copy(bias[:, :, :], bias_all[:, :, 0:2]).then_inc(s_bp, 1)
                    dve.wait_ge(s_bo, 17)

                    def proj(i, g):
                        dve.wait_ge(s_proj, PROJ * i + g + 1)
                        b = g % RING
                        if g < 8:
                            dve.tensor_scalar(proj_out(g, None), bank[b][:, :],
                                              bias[:, g // 4, (g // 2) % 2:(g // 2) % 2 + 1], None,
                                              ALU.add).then_inc(s_pv, 1)
                        else:
                            dve.tensor_copy(proj_out(g, None), bank[b][:, :]).then_inc(s_pv, 1)

                    def masked(i, u):
                        b = u % NS
                        at = U * i + u
                        dve.wait_ge(s_sc, at + 1)
                        dve.scalar_tensor_tensor(s[b][:, :], bank[3 + u % 2][:, 0:3 * P], -INV_SCALE,
                                                 cst[:, C_MASK:C_MASK + 3 * P], ALU.mult, ALU.max).then_inc(s_sm, 1)
                        dve.wait_ge(s_sm, at + 1)
                        for t, cols in ((0, slice(0, P)), (1, slice(P, 3 * P))):
                            dve.tensor_reduce(mn[:, b, t:t + 1], s[b][:, cols], op=ALU.min,
                                              axis=AX.X).then_inc(s_mn, 1)

                    def recip(i, u):
                        b = u % NS
                        dve.wait_ge(s_e, 2 * (U * i + u + 1))
                        dve.reciprocal(rr[:, b, :], rs[:, b, :]).then_inc(s_rr, 1)

                    def z_low(i, u):
                        bt, h = unit(u)
                        cols = slice(bt * SEQ, (bt + 1) * SEQ)
                        dve.wait_ge(s_zh, U * i + u + 1)
                        dve.scalar_tensor_tensor(zT_l[:, h, cols], bank[7][:, 0:SEQ],
                                                 bias[:, 2, h:h + 1], zT_h[:, h, cols].bitcast(FP32),
                                                 ALU.add, ALU.subtract).then_inc(s_zl, 1)

                    def added(i, bt):
                        dve.wait_ge(s_o, BATCH * i + bt + 1)
                        r = x_res[:, 2 * bt:2 * bt + 2, :].rearrange("p a b -> p (a b)")
                        dve.tensor_tensor(r, r, bank[bt % RING][:, :], ALU.add).then_inc(s_ov, 1)

                    def body(i):
                        dve.wait_ge(s_bp, i + 1)
                        for g in range(1, PROJ, 2):
                            proj(i, g)
                        masked(i, 0)
                        masked(i, 1)
                        recip(i, 0)
                        masked(i, 2)
                        recip(i, 1)
                        for u in range(U):
                            if u + 3 < U:
                                masked(i, u + 3)
                            if u + 2 < U:
                                recip(i, u + 2)
                            z_low(i, u)
                            if u >= 5:
                                added(i, u - 5)
                        added(i, 3)

                    with dve.Fori(0, NP - 1) as i:
                        body(i)
                        dve.tensor_copy(bias[:, :, :], bias_all[:, :, bass.ds(2 * i + 2, 2)]).then_inc(s_bp, 1)
                    body(NP - 1)

                @block.tensor
                def _(pe):
                    norm_transposes(pe, n)
                    pe.wait_ge(n["xth"], 4)
                    pe.wait_ge(n["xtl"], 4)

                    def proj(i, g, fresh):
                        b = g % RING
                        if g >= RING:
                            o = g - RING
                            if o % 2 == 0:
                                pe.wait_ge(s_pa, (PROJ // 2) * i + o // 2 + 1)
                            else:
                                pe.wait_ge(s_pv, (PROJ // 2) * i + o // 2 + 1)
                        elif not fresh and g == 0:
                            pe.wait_ge(s_ov, BATCH * i)
                        for k in range(KD):
                            if g < 8:
                                t, h, half = g // 4, (g // 2) % 2, g % 2
                                toks = slice(half * HALF, (half + 1) * HALF)
                                w = slice(h * DH, (h + 1) * DH)
                                last = split_matmuls(pe, bank[b][:, :], (w_h[:, t, k, w], w_l[:, t, k, w]),
                                                     (xT_h[:, k, toks], xT_l[:, k, toks]), k == 0, k == KD - 1)
                        if g >= 8:
                            for j in range(2):
                                toks = slice((2 * (g - 8) + j) * P, (2 * (g - 8) + j + 1) * P)
                                for k in range(KD):
                                    last = split_matmuls(pe, bank[b][:, j * 2 * DH:(j + 1) * 2 * DH],
                                                         (xT_h[:, k, toks], xT_l[:, k, toks]),
                                                         (w_h[:, 2, k, :], w_l[:, 2, k, :]), k == 0, k == KD - 1)
                        last.then_inc(s_proj, 1)

                    def scores(i, u):
                        bt, h = unit(u)
                        b = bank[3 + u % 2]
                        if u == 0:
                            pe.wait_ge(s_pa, (PROJ // 2) * (i + 1))
                            pe.wait_ge(s_pv, (PROJ // 2) * (i + 1))
                        if u >= 2:
                            pe.wait_ge(s_sm, U * i + u - 1)
                        q, k = qk[:, 0, h, :], qk[:, 1, h, :]
                        t0 = bt * SEQ
                        pe.matmul(b[:, 0:P], q[:, t0:t0 + P], k[:, t0:t0 + P], start=True, stop=True)
                        pe.matmul(b[:, P:3 * P], q[:, t0 + P:t0 + 2 * P], k[:, t0:t0 + 2 * P],
                                  start=True, stop=True).then_inc(s_sc, 1)

                    def turn(i, u):
                        pe.wait_ge(s_p, 2 * (U * i + u + 1))
                        if u >= 2:
                            pe.wait_ge(s_ptv, U * i + u - 1)
                        for c in range(3):
                            last = pe.transpose(bank[5 + u % 2][:, c * P:(c + 1) * P],
                                                s[u % NS][:, c * P:(c + 1) * P], ident)
                        last.then_inc(s_pt, 1)

                    def mix(i, u):
                        bt, h = unit(u)
                        pe.wait_ge(s_ptv, U * i + u + 1)
                        if u >= 1:
                            pe.wait_ge(s_zl, U * i + u)
                        e = slice(h * DH, (h + 1) * DH)
                        pe.matmul(bank[7][:, 0:2 * P], v[:, 2 * bt, e], pT[u % 2][:, 0:2 * P], start=True, stop=False)
                        pe.matmul(bank[7][:, P:2 * P], v[:, 2 * bt + 1, e], pT[u % 2][:, 2 * P:3 * P],
                                  start=False, stop=True).then_inc(s_z, 1)

                    def project(i, bt):
                        pe.wait_ge(s_zh, U * i + 2 * bt + 2)
                        pe.wait_ge(s_zl, U * i + 2 * bt + 2)
                        if bt == 0:
                            pe.wait_ge(s_wol, i + 1)
                        if bt >= RING:
                            pe.wait_ge(s_ov, BATCH * i + bt - RING + 1)
                        for j in range(2):
                            toks = slice((2 * bt + j) * P, (2 * bt + j + 1) * P)
                            for h in range(2):
                                last = split_matmuls(pe, bank[bt % RING][:, j * D:(j + 1) * D],
                                                     (zT_h[:, h, toks], zT_l[:, h, toks]),
                                                     (wo_h[:, h, :], wo_l[:, h, :]), h == 0, h == 1)
                        last.then_inc(s_o, 1)

                    def body(i, fresh):
                        pe.wait_ge(s_wl, i + 1)
                        for g in range(PROJ):
                            proj(i, g, fresh)
                        scores(i, 0)
                        scores(i, 1)
                        scores(i, 2)
                        for u in range(U):
                            turn(i, u)
                            if u + 3 < U:
                                scores(i, u + 3)
                            if u >= 5:
                                project(i, u - 5)
                            mix(i, u)
                        project(i, 3)

                    body(0, True)
                    with pe.Fori(1, NP) as i:
                        body(i, False)

                block_ctx.close()

        ffn("f0", True)
        attention()
        ffn("f1", False)


def kernel(**inputs):
    import concourse.bacc as bacc
    from concourse.bass_utils import run_bass_kernel_spmd

    def chunks(w, rows, p):
        w = w.reshape(*w.shape[:-2], rows // p, p, w.shape[-1])
        return np.moveaxis(w, -2, 0)

    a = {k.removeprefix("L0_"): np.asarray(v) for k, v in inputs.items()}
    gu = a["ffn_shared_gate_up_w"].reshape(2, ISH, D)
    gu = np.concatenate([gu, np.zeros((2, ISP - ISH, D), np.float32)], 1).reshape(2 * ISP, D)
    dn = np.concatenate([a["ffn_shared_down_w"], np.zeros((D, ISP - ISH), np.float32)], 1)
    gate = np.concatenate([a["ffn_gate_w"], a["ffn_shared_gate_w"], a["ffn_shared_gate_w"]], 0)

    def heads(w):
        w = w.reshape(NP, 2, KD, P, DH)
        return w.transpose(0, 3, 2, 1, 4)

    arrays = {
        "x_in": a["attn_x"].reshape(TOK, D),
        "consts": constants(),
        "wgate": chunks(gate.T, D, P).reshape(P, KD * NG),
        "wgu": chunks(gu.T, D, P),
        "wd": chunks(dn.T, ISP, P),
        "w1": chunks(a["ffn_w1"].transpose(0, 2, 1), D, P),
        "w2": chunks(a["ffn_w2"].transpose(0, 2, 1), IM, IC),
        "wqkv": np.stack([heads(a[f"attn_W_{t}"]) for t in "QKV"], 2).reshape(NP, P, -1),
        "wo": a["attn_W_O"].reshape(NP, 2, DH, D).transpose(0, 2, 1, 3).reshape(NP, P, 2 * D),
        "bqkv": np.stack([a[f"attn_b_{t}"].T for t in "QKV"], 1),
        "bo": a["attn_b_O"],
    }
    nc = bacc.Bacc("TRN2", target_bir_lowering=False, num_devices=1)
    ins, aps = {}, {}
    for name, arr in arrays.items():
        arr = np.ascontiguousarray(arr)
        ins[f"in_{name}"] = arr
        aps[name] = nc.dram_tensor(f"in_{name}", arr.shape, mybir.dt.from_np(arr.dtype), kind="ExternalInput").ap()
    aps["out"] = nc.dram_tensor("out_0", (TOK, D), FP32, kind="ExternalOutput").ap()
    macaron(nc, **aps)
    r = run_bass_kernel_spmd(nc, [ins], core_ids=[0])
    return r.results[0]["out_0"].reshape(BATCH, SEQ, D)
```

```python
import numpy as np
import concourse.bass as bass
from concourse import mybir
from contextlib import ExitStack

FP32 = mybir.dt.float32
FP32R = mybir.dt.float32r
BF16 = mybir.dt.bfloat16
I32 = mybir.dt.int32
ALU = mybir.AluOpType
ACT = mybir.ActivationFunctionType
AX = mybir.AxisListType

P = 128
BATCH, SEQ, D = 4, 256, 256
TOK = BATCH * SEQ
NT = TOK // P
KD = D // P
HALF = 512
NE = 8
TOP_K = 2
IM = 176
IC = IM // 2
ISH = 704
SC = -(-ISH // P)
ISP = SC * P
NG = NE + 1
NH, DH = 16, 128
NP = NH // 2
NM = TOP_K * NT + NE - 1
NST = 3
EPS = 1e-5
IGNORE = -100000.0
BIG = 3.0e38
INV_SCALE = 1.0 / float(np.sqrt(np.float32(DH)))

POOL_JOBS_FIRST = (4, 5, 7, 10, 13)
POOL_JOBS_SECOND = (1, 4)
ZFILL_AFTER = 8

C_ID = 0
C_U = C_ID + P
C_ONE = C_U + P
C_MASK = C_ONE + P
C_DESC = C_MASK + 3 * P
C_M128 = C_DESC + NE
C_LT = C_M128 + NT
C_MI = C_LT + NE * NE
C_EPS = C_MI + NM
C_NH = C_EPS + NT
C_ZERO = C_NH + NT
C_N = C_ZERO + 1


def constants():
    c = np.zeros((P, C_N), np.float32)
    r = np.arange(P)
    c[:, C_ID:C_ID + P] = np.eye(P)
    c[:, C_U:C_U + P] = r[:, None] < r[None, :]
    c[:, C_ONE:C_ONE + P] = 1.0
    diagonal = np.where(r[None, :] <= r[:, None], -BIG, -IGNORE)
    c[:, C_MASK:C_MASK + P] = diagonal
    c[:, C_MASK + P:C_MASK + 2 * P] = -BIG
    c[:, C_MASK + 2 * P:C_MASK + 3 * P] = diagonal
    c[:, C_DESC:C_DESC + NE] = NE - np.arange(NE)
    c[:, C_M128:C_M128 + NT] = P * np.arange(NT)
    e = np.arange(NE)
    c[:, C_LT:C_LT + NE * NE] = (e[None, :] < e[:, None]).reshape(-1)
    c[:, C_MI:C_MI + NM] = np.arange(NM)
    c[:, C_EPS:C_EPS + NT] = EPS
    c[:, C_NH:C_NH + NT] = -0.5
    return c


def macaron(nc, x_in, consts, wgate, wgu, wd, w1, w2, wqkv, wo, bqkv, bo, out):
    ctx = ExitStack()
    with ctx:
        def sbuf(name, shape, dt=FP32, stack=ctx):
            return stack.enter_context(nc.sbuf_tensor(name, shape, dt))

        def sem(name):
            return ctx.enter_context(nc.semaphore(name))

        xg = nc.dram_tensor("x_by_expert", (NM * P, D), FP32, kind="Internal").ap()
        yg = nc.dram_tensor("y_by_expert", (NM * P, D), FP32, kind="Internal").ap()

        cst = sbuf("cst", [P, C_N])
        x_res = sbuf("x_res", [P, NT, D])
        xn = sbuf("xn", [P, NT, D])
        xT_h = sbuf("xT_h", [P, KD, TOK], FP32R)
        xT_l = sbuf("xT_l", [P, KD, TOK], FP32R)
        wg_h = sbuf("wg_h", [P, KD, P], FP32R)
        wg_l = sbuf("wg_l", [P, KD, P], FP32R)
        wgu_h = sbuf("wgu_h", [P, KD, 2 * ISP], FP32R)
        wgu_l = sbuf("wgu_l", [P, KD, 2 * ISP], FP32R)
        wd_h = sbuf("wd_h", [P, SC, D], FP32R)
        wd_l = sbuf("wd_l", [P, SC, D], FP32R)
        w1_h = sbuf("w1_h", [P, NE, KD, 2 * IM], FP32R)
        w1_l = sbuf("w1_l", [P, NE, KD, 2 * IM], FP32R)
        rank_w = sbuf("rank_w", [P, 2, P], BF16)
        stats = sbuf("stats", [P, NT, 6])
        mv = sbuf("mv", [P, NT, 2])
        rstd = sbuf("rstd", [P, NT])
        bank = [ctx.enter_context(nc.psum_tensor(f"bank{b}", [P, HALF], FP32)) for b in range(8)]
        ident = cst[:, C_ID:C_ID + P]
        s_gath = [sem(f"s_gath{b}") for b in range(NT)]

        def split_matmuls(pe, psum, lhs, rhs, first, last):
            pe.matmul(psum, lhs[0], rhs[0], start=first, stop=False)
            pe.matmul(psum, lhs[0], rhs[1], start=False, stop=False)
            return pe.matmul(psum, lhs[1], rhs[0], start=False, stop=last)

        def norm_stats(dve, s, tag_wait):
            for j in range(NT):
                if tag_wait is not None:
                    dve.wait_ge(tag_wait[j], 16)
                dve.bn_stats(stats[:, j, :], x_res[:, j, :]).then_inc(s["stats"], 1)
            for j in range(NT):
                dve.wait_ge(s["stats"], j + 1)
                dve.bn_aggr(mv[:, j, :], stats[:, j, :]).then_inc(s["mv"], 1)

        def norm_apply(dve, s):
            dve.wait_ge(s["rstd"], 2)
            for j in range(NT):
                dve.tensor_scalar(xn[:, j, :], x_res[:, j, :], mv[:, j, 0:1], rstd[:, j:j + 1],
                                  ALU.subtract, ALU.mult).then_inc(s["xn"], 1)

        def norm_rstd(pool, s):
            pool.wait_ge(s["mv"], NT)
            pool.tensor_tensor(rstd[:, :], mv[:, :, 1], cst[:, C_EPS:C_EPS + NT], ALU.add).then_inc(s["rstd"], 1)
            pool.wait_ge(s["rstd"], 1)
            pool.tensor_tensor(rstd[:, :], rstd[:, :], cst[:, C_NH:C_NH + NT], ALU.pow).then_inc(s["rstd"], 1)

        def norm_transposes(pe, s):
            for g in range(4):
                half, k = divmod(g, KD)
                pe.wait_ge(s["xn"], 4 * half + 4)
                for j in range(4):
                    last = pe.transpose(bank[g][:, j * P:(j + 1) * P],
                                        xn[:, 4 * half + j, k * P:(k + 1) * P], ident)
                last.then_inc(s["xt"], 1)

        def norm_split_high(act, s):
            for g in range(4):
                half, k = divmod(g, KD)
                act.wait_ge(s["xt"], g + 1)
                act.activation(xT_h[:, k, half * HALF:(half + 1) * HALF], bank[g][:, :],
                               ACT.Copy).then_inc(s["xth"], 1)

        def norm_split_low(dve, s):
            for g in range(4):
                half, k = divmod(g, KD)
                cols = slice(half * HALF, (half + 1) * HALF)
                dve.wait_ge(s["xth"], g + 1)
                dve.tensor_tensor(xT_l[:, k, cols], bank[g][:, :], xT_h[:, k, cols].bitcast(FP32),
                                  ALU.subtract).then_inc(s["xtl"], 1)

        def norm_sems(tag):
            return {n: sem(f"{n}_{tag}") for n in ("stats", "mv", "rstd", "xn", "xt", "xth", "xtl")}

        def ffn(tag, first):
            loc = ExitStack()
            with loc:
                def sb(name, shape, dt=FP32):
                    return sbuf(f"{name}_{tag}", shape, dt, loc)

                w2_h = sb("w2_h", [IC, NE, 2, D], FP32R)
                w2_l = sb("w2_l", [IC, NE, 2, D], FP32R)
                stage = [sb(f"stage{b}", [P, ISP]) for b in range(NST)]
                wg_raw = sb("wg_raw", [P, KD * P])
                hs = [sb(f"hs{b}", [P, HALF]) for b in range(2)]
                hT_h = sb("hT_h", [P, SC, HALF], FP32R)
                hT_l = sb("hT_l", [P, SC, HALF], FP32R)
                xe = [sb(f"xe{b}", [P, D]) for b in range(2)]
                xeT_h = [sb(f"xeT_h{b}", [P, KD * P], FP32R) for b in range(2)]
                xeT_l = [sb(f"xeT_l{b}", [P, KD * P], FP32R) for b in range(2)]
                he = [sb(f"he{b}", [P, IM]) for b in range(2)]
                heT_h = [sb(f"heT_h{b}", [IC, 2 * P], FP32R) for b in range(2)]
                heT_l = [sb(f"heT_l{b}", [IC, 2 * P], FP32R) for b in range(2)]
                ye = [sb(f"ye{b}", [P, D]) for b in range(2)]
                lgT = hs
                lg = sb("lg", [P, NT, NG])
                dl = sb("dl", [P, NT, NE])
                sc = sb("sc", [P, NT, NE])
                sel = [sb(f"sel{b}", [P, NT, NE]) for b in range(TOP_K)]
                assigned = sb("assigned", [P, NT * NE], BF16)
                best = sb("best", [P, NT])
                best2 = sb("best2", [P, NT])
                lead = sb("lead", [P, NT])
                rank = sb("rank", [P, 2, NT, NE])
                cum = sb("cum", [P, NT + 1, NE])
                cmp = sb("cmp", [P, NE, NE])
                tiles_of = sb("tiles_of", [P, NE])
                base = sb("base", [P, NE])
                end = sb("end", [P, NE])
                slot = sb("slot", [P, NT, NE])
                slot_f = sb("slot_f", [P, TOP_K, NT])
                slot_i = sb("slot_i", [P, TOP_K * NT], I32)
                tile_cmp = sb("tile_cmp", [1, NM, NE])
                tile_f = sb("tile_f", [1, NM])
                tile_e = sb("tile_e", [1, NM], I32)
                gates = sb("gates", [P, 2, NT])
                gates_r = sb("gates_r", [P, 2, NT])
                cw2 = sb("cw2", [P, NT])

                n = norm_sems(tag)
                s_x = [sem(f"s_x{j}_{tag}") for j in range(NT)] if first else None
                if first:
                    s_cst, s_rw = sem("s_cst"), sem("s_rank_weights")
                    s_gate_in, s_gh, s_gl = sem("s_gate_in"), sem("s_gate_high"), sem("s_gate_low")
                    s_zero, s_zfill = sem("s_zero"), sem("s_zero_fill")
                s_stage = [sem(f"s_stage{b}_{tag}") for b in range(NST)]
                s_wh = sem(f"s_wh_{tag}")
                s_wl = sem(f"s_wl_{tag}")
                s_wlp = sem(f"s_wlp_{tag}")
                s_lgt = sem(f"s_lgt_{tag}")
                s_lgt_sb = sem(f"s_lgt_sb_{tag}")
                s_logits = sem(f"s_logits_{tag}")
                s_route = sem(f"s_route_{tag}")
                s_exp = sem(f"s_exp_{tag}")
                s_assigned = sem(f"s_assigned_{tag}")
                s_rank = sem(f"s_rank_{tag}")
                s_rank_sb = sem(f"s_rank_sb_{tag}")
                s_slot = sem(f"s_slot_{tag}")
                s_expert = sem(f"s_expert_{tag}")
                s_scat = sem(f"s_scat_{tag}")
                s_up = sem(f"s_up_{tag}")
                s_silu = sem(f"s_silu_{tag}")
                s_hm = sem(f"s_hm_{tag}")
                s_hh = sem(f"s_hh_{tag}")
                s_hl = sem(f"s_hl_{tag}")
                s_dn = sem(f"s_dn_{tag}")
                s_dnv = sem(f"s_dnv_{tag}")
                s_xe = [sem(f"s_xe{b}_{tag}") for b in range(2)]
                s_tx = sem(f"s_tx_{tag}")
                s_txh = sem(f"s_txh_{tag}")
                s_txl = sem(f"s_txl_{tag}")
                s_eu = sem(f"s_eu_{tag}")
                s_es = sem(f"s_es_{tag}")
                s_em = sem(f"s_em_{tag}")
                s_th = sem(f"s_th_{tag}")
                s_thh = sem(f"s_thh_{tag}")
                s_thl = sem(f"s_thl_{tag}")
                s_ed = sem(f"s_ed_{tag}")
                s_ye = sem(f"s_ye_{tag}")
                s_yst = [sem(f"s_yst{b}_{tag}") for b in range(2)]
                s_add = sem(f"s_add_{tag}")
                s_out = None if first else sem("s_out")

                jobs = []
                if first:
                    for g in range(2):
                        for k in range(KD):
                            cols = slice(g * ISP, (g + 1) * ISP)
                            jobs.append((wgu[:, k, cols], wgu_h[:, k, cols], wgu_l[:, k, cols]))
                    for a in range(0, SC, 3):
                        jobs.append((wd[:, a:a + 3, :], wd_h[:, a:a + 3, :], wd_l[:, a:a + 3, :]))
                    early = len(jobs)
                    for e in range(NE):
                        jobs.append((w1[:, e], w1_h[:, e], w1_l[:, e]))
                else:
                    early = 0
                for e in range(NE):
                    jobs.append((w2[:, e], w2_h[:, e], w2_l[:, e]))
                before_up = min(4, early)
                by_pool = set(POOL_JOBS_FIRST if first else POOL_JOBS_SECOND)

                def lows(q, pool_side):
                    return sum((r in by_pool) == pool_side for r in range(q + 1))

                def wait_low(eng, q):
                    if lows(q, False):
                        eng.wait_ge(s_wl, lows(q, False))
                    if lows(q, True):
                        eng.wait_ge(s_wlp, lows(q, True))


                def flat(ap):
                    return ap.rearrange("p a b -> p (a b)") if len(ap.shape) == 3 else ap

                def job_high(act, q):
                    src, high, _ = jobs[q]
                    act.wait_ge(s_stage[q % NST], 16 * (q // NST + 1))
                    rows, cols = flat(high).shape
                    act.activation(flat(high), stage[q % NST][0:rows, 0:cols], ACT.Copy).then_inc(s_wh, 1)

                def job_low(eng, q, done):
                    _, high, low = jobs[q]
                    eng.wait_ge(s_wh, q + 1)
                    rows, cols = flat(high).shape
                    eng.tensor_tensor(flat(low), stage[q % NST][0:rows, 0:cols], flat(high).bitcast(FP32),
                                      ALU.subtract).then_inc(done, 1)

                late = list(range(early, len(jobs)))
                share = -(-len(late) // SC)
                late_of = [late[c * share:(c + 1) * share] for c in range(SC)]

                block_ctx = ExitStack()
                block = block_ctx.enter_context(nc.Block())

                @block.sync
                def _(sp):
                    if first:
                        xv = x_in.rearrange("(j p) d -> p j d", p=P)
                        sp.dma_start(x_res[:, 0, :], xv[:, 0, :]).then_inc(s_x[0], 16)
                        sp.dma_start(cst[:, :], consts).then_inc(s_cst, 16)
                        for j in range(1, NT):
                            sp.dma_start(x_res[:, j, :], xv[:, j, :]).then_inc(s_x[j], 16)
                        sp.dma_start(wg_raw[:, :], wgate).then_inc(s_gate_in, 16)
                    for q, (src, high, _) in enumerate(jobs):
                        if q >= NST:
                            wait_low(sp, q - NST)
                        rows, cols = flat(high).shape
                        sp.dma_start(stage[q % NST][0:rows, 0:cols], flat(src)).then_inc(s_stage[q % NST], 16)
                        if first and q == ZFILL_AFTER:
                            sp.wait_ge(s_zero, 1)
                            sp.dma_start(xg.rearrange("(m p) d -> p m d", p=P),
                                         ye[0][:, :].unsqueeze(1).to_broadcast([P, NM, D])).then_inc(s_zfill, 16)

                    def load(m, q, b):
                        sp.dma_start(xe[b][:, :], xg[bass.ds(m * P, P), :]).then_inc(s_xe[b], 16)

                    sp.wait_ge(s_scat, 16 * TOP_K * NT)
                    load(0, 0, 0)
                    load(1, 0, 1)
                    with sp.Fori(0, (NM - 3) // 2) as i:
                        for b in range(2):
                            sp.wait_ge(s_tx, 2 * i + b + 1)
                            load(2 * i + 2 + b, i + 1, b)
                    sp.wait_ge(s_tx, NM - 2)
                    load(NM - 1, (NM - 1) // 2, 0)
                    if not first:
                        ov = out.rearrange("(j p) d -> p j d", p=P)
                        for j in range(NT):
                            sp.wait_ge(s_add, TOP_K * (j + 1))
                            sp.wait_ge(s_dnv, j + 1)
                            sp.dma_start(ov[:, j, :], x_res[:, j, :]).then_inc(s_out, 16)
                        sp.wait_ge(s_out, 16 * NT)

                @block.gpsimd
                def _(pool):
                    if first:
                        pool.memset(ye[0][:, :], 0.0).then_inc(s_zero, 1)
                        pool.wait_ge(s_cst, 16)
                    norm_rstd(pool, n)
                    for q in sorted(by_pool):
                        job_low(pool, q, s_wlp)
                    pool.wait_ge(n["xn"], NT)
                    pool.wait_ge(s_slot, 1)
                    if first:
                        pool.wait_ge(s_zfill, 16)
                    for j in range(NT):
                        for t in range(TOP_K):
                            col = t * NT + j
                            pool.indirect_dma_start(
                                xg, bass.IndirectOffsetOnAxis(ap=slot_i[:, col:col + 1], axis=0),
                                xn[:, j, :], None).then_inc(s_scat, 16)

                    def store(m, b):
                        pool.wait_ge(s_ye, m + 1)
                        pool.dma_start(yg[bass.ds(m * P, P), :], ye[b][:, :]).then_inc(s_yst[b], 16)

                    with pool.Fori(0, (NM - 1) // 2) as i:
                        for b in range(2):
                            store(2 * i + b, b)
                    store(NM - 1, 0)
                    pool.wait_ge(s_yst[0], 16 * ((NM + 1) // 2))
                    pool.wait_ge(s_yst[1], 16 * (NM // 2))
                    pool.wait_ge(s_scat, 16 * TOP_K * NT)
                    for g in range(TOP_K * NT):
                        j, t = divmod(g, TOP_K)
                        if g >= NT:
                            pool.wait_ge(s_add, g - NT + 1)
                        col = t * NT + j
                        pool.indirect_dma_start(
                            xn[:, g % NT, :], None, yg,
                            bass.IndirectOffsetOnAxis(ap=slot_i[:, col:col + 1], axis=0)).then_inc(s_gath[g % NT], 16)

                @block.scalar
                def _(act):
                    if first:
                        for q in range(before_up):
                            job_high(act, q)
                        act.wait_ge(s_gate_in, 16)
                        act.activation(flat(wg_h[:, :, :]), wg_raw[:, :], ACT.Copy).then_inc(s_gh, 1)
                    norm_split_high(act, n)
                    for half in range(2):
                        act.wait_ge(s_lgt, half + 1)
                        act.activation(lgT[half][0:NG, :], bank[5 + half][0:NG, :], ACT.Copy).then_inc(s_lgt_sb, 1)
                    act.wait_ge(s_route, 8)
                    act.activation(gates[:, 0, :], best2[:, :], ACT.Exp).then_inc(s_exp, 1)
                    act.activation(gates[:, 1, :], lg[:, :, NE], ACT.Exp, scale=-1.0).then_inc(s_exp, 1)

                    def shared_silu(c):
                        act.wait_ge(s_up, c + 1)
                        if c >= 2:
                            act.wait_ge(s_hl, c - 1)
                        act.activation(hs[c % 2][:, :], bank[2 * (c % 2)][:, :], ACT.Silu).then_inc(s_silu, 1)

                    def shared_high(c):
                        act.wait_ge(s_hm, c + 1)
                        act.activation(hT_h[:, c % SC, :], hs[c % 2][:, :], ACT.Copy).then_inc(s_hh, 1)

                    for c in range(SC):
                        if c == 0:
                            act.wait_ge(s_logits, 1)
                        shared_silu(c)
                        if c == 0:
                            for q in range(before_up, early):
                                job_high(act, q)
                        if c == 1:
                            act.wait_ge(s_rank, 1)
                            act.activation(rank[:, :, :, :].rearrange("p a b c -> p (a b c)"),
                                           bank[5][:, 0:2 * NT * NE], ACT.Copy).then_inc(s_rank_sb, 1)
                        for q in late_of[c]:
                            job_high(act, q)
                        shared_high(c)

                    def tile_high(m, b):
                        act.wait_ge(s_tx, m + 1)
                        act.activation(xeT_h[b][:, :], bank[b][:, 0:KD * P], ACT.Copy).then_inc(s_txh, 1)

                    def inner_high(m, b):
                        act.wait_ge(s_th, m + 1)
                        act.activation(heT_h[b][:, :], bank[4 + b][0:IC, 0:2 * P], ACT.Copy).then_inc(s_thh, 1)

                    def inner_silu(m, b):
                        act.wait_ge(s_eu, m + 1)
                        act.activation(he[b][:, :], bank[2 + b][:, 0:IM], ACT.Silu).then_inc(s_es, 1)

                    def tile_out(m, q, b, guard=True):
                        act.wait_ge(s_ed, m + 1)
                        if guard:
                            act.wait_ge(s_yst[b], 16 * q)
                        act.activation(ye[b][:, :], bank[6 + b][:, 0:D], ACT.Copy).then_inc(s_ye, 1)

                    def step(m, q, b, guard=True):
                        tile_high(m + 1, 1 - b)
                        inner_silu(m, b)
                        inner_high(m - 1, 1 - b)
                        tile_out(m - 2, q - 1, b, guard)

                    tile_high(0, 0)
                    tile_high(1, 1)
                    inner_silu(0, 0)
                    tile_high(2, 0)
                    inner_silu(1, 1)
                    inner_high(0, 0)
                    step(2, 1, 0, False)
                    step(3, 1, 1, False)
                    with act.Fori(2, NM // 2) as i:
                        step(2 * i, i, 0)
                        step(2 * i + 1, i, 1)
                    m = NM - 1
                    inner_silu(m, 0)
                    inner_high(m - 1, 1)
                    tile_out(m - 2, m // 2 - 1, 0)
                    inner_high(m, 0)
                    tile_out(m - 1, m // 2 - 1, 1)
                    tile_out(m, m // 2, 0)
                    for c in range(SC, 2 * SC):
                        shared_silu(c)
                        shared_high(c)

                @block.vector
                def _(dve):
                    steps = [0]

                    def link(ins):
                        steps[0] += 1
                        ins.then_inc(s_route, 1)
                        dve.wait_ge(s_route, steps[0])

                    norm_stats(dve, n, s_x)
                    norm_apply(dve, n)
                    for q in range(before_up):
                        job_low(dve, q, s_wl)
                    if first:
                        dve.wait_ge(s_gh, 1)
                        dve.tensor_tensor(flat(wg_l[:, :, :]), wg_raw[:, :], flat(wg_h[:, :, :]).bitcast(FP32),
                                          ALU.subtract).then_inc(s_gl, 1)
                        dve.tensor_copy(rank_w[:, :, :].rearrange("p a b -> p (a b)"),
                                        cst[:, C_U:C_ONE + P]).then_inc(s_rw, 1)
                    norm_split_low(dve, n)

                    def wide(ap):
                        return ap.unsqueeze(2).to_broadcast([P, NT, NE])

                    desc = cst[:, C_DESC:C_DESC + NE].unsqueeze(1).to_broadcast([P, NT, NE])
                    dve.wait_ge(s_logits, 1)
                    link(dve.tensor_copy(flat(lg[:, :, :]), bank[4][:, 0:NT * NG]))
                    link(dve.tensor_reduce(best[:, :], lg[:, :, 0:NE], op=ALU.max, axis=AX.X))
                    link(dve.tensor_tensor(dl[:, :, :], lg[:, :, 0:NE], wide(best[:, :]), ALU.subtract))
                    link(dve.scalar_tensor_tensor(sc[:, :, :], dl[:, :, :], 0.0, desc, ALU.is_ge, ALU.mult))
                    link(dve.tensor_reduce(lead[:, :], sc[:, :, :], op=ALU.max, axis=AX.X))
                    link(dve.tensor_tensor(sel[0][:, :, :], sc[:, :, :], wide(lead[:, :]), ALU.is_equal))
                    link(dve.scalar_tensor_tensor(dl[:, :, :], sel[0][:, :, :], -BIG, dl[:, :, :], ALU.mult, ALU.add))
                    link(dve.tensor_reduce(best2[:, :], dl[:, :, :], op=ALU.max, axis=AX.X))
                    link(dve.tensor_tensor(dl[:, :, :], dl[:, :, :], wide(best2[:, :]), ALU.is_equal))
                    link(dve.tensor_tensor(sc[:, :, :], dl[:, :, :], desc, ALU.mult))
                    link(dve.tensor_reduce(lead[:, :], sc[:, :, :], op=ALU.max, axis=AX.X))
                    link(dve.tensor_tensor(sel[1][:, :, :], sc[:, :, :], wide(lead[:, :]), ALU.is_equal))
                    dve.tensor_tensor(assigned[:, :], flat(sel[0][:, :, :]), flat(sel[1][:, :, :]),
                                      ALU.add).then_inc(s_assigned, 1)

                    def shared_mul(c):
                        dve.wait_ge(s_silu, c + 1)
                        dve.tensor_tensor(hs[c % 2][:, :], hs[c % 2][:, :], bank[2 * (c % 2) + 1][:, :],
                                          ALU.mult).then_inc(s_hm, 1)

                    def shared_low(c):
                        dve.wait_ge(s_hh, c + 1)
                        dve.tensor_tensor(hT_l[:, c % SC, :], hs[c % 2][:, :], hT_h[:, c % SC, :].bitcast(FP32),
                                          ALU.subtract).then_inc(s_hl, 1)

                    def shared_out(j):
                        dve.wait_ge(s_dn, j + 1)
                        dve.scalar_tensor_tensor(x_res[:, j, :], bank[6 + j % 2][:, 0:D], gates_r[:, 1, j:j + 1],
                                                 x_res[:, j, :], ALU.mult, ALU.add).then_inc(s_dnv, 1)

                    def slots():
                        link(dve.memset(cum[:, 0, :], 0.0))
                        dve.wait_ge(s_rank_sb, 1)
                        for j in range(NT):
                            link(dve.tensor_tensor(cum[:, j + 1, :], cum[:, j, :], rank[:, 1, j, :], ALU.add))
                        link(dve.tensor_tensor(cmp[:, :, :], wide(cum[:, NT, :]),
                                               cst[:, C_M128:C_M128 + NT].unsqueeze(1).to_broadcast([P, NE, NT]),
                                               ALU.is_gt))
                        link(dve.tensor_reduce(tiles_of[:, :], cmp[:, :, :], op=ALU.add, axis=AX.X))
                        link(dve.tensor_tensor(cmp[:, :, :], tiles_of[:, :].unsqueeze(1).to_broadcast([P, NE, NE]),
                                               cst[:, C_LT:C_LT + NE * NE].rearrange("p (a b) -> p a b", a=NE),
                                               ALU.mult))
                        link(dve.tensor_reduce(base[:, :], cmp[:, :, :], op=ALU.add, axis=AX.X))
                        link(dve.tensor_tensor(slot[:, :, :], rank[:, 0], cum[:, 0:NT, :], ALU.add))
                        link(dve.scalar_tensor_tensor(slot[:, :, :],
                                                      base[:, :].unsqueeze(1).to_broadcast([P, NT, NE]), float(P),
                                                      slot[:, :, :], ALU.mult, ALU.add))
                        for t in range(TOP_K):
                            link(dve.tensor_tensor(sel[t][:, :, :], sel[t][:, :, :], slot[:, :, :], ALU.mult))
                            link(dve.tensor_reduce(slot_f[:, t, :], sel[t][:, :, :], op=ALU.add, axis=AX.X))
                        dve.tensor_copy(slot_i[:, :], flat(slot_f[:, :, :])).then_inc(s_slot, 1)
                        link(dve.tensor_tensor(end[:, :], base[:, :], tiles_of[:, :], ALU.add))
                        link(dve.tensor_tensor(tile_cmp[0:1, :, :],
                                               cst[0:1, C_MI:C_MI + NM].unsqueeze(2).to_broadcast([1, NM, NE]),
                                               end[0:1, :].unsqueeze(1).to_broadcast([1, NM, NE]), ALU.is_ge))
                        link(dve.tensor_reduce(tile_f[0:1, :], tile_cmp[0:1, :, :], op=ALU.add, axis=AX.X))
                        dve.tensor_scalar(tile_e[0:1, :], tile_f[0:1, :], float(NE - 1), None,
                                          ALU.min).then_inc(s_expert, 1)

                    def weights():
                        dve.wait_ge(s_exp, 2)
                        link(dve.tensor_scalar(gates_r[:, :, :], gates[:, :, :], 1.0, None, ALU.add))
                        link(dve.reciprocal(gates_r[:, :, :], gates_r[:, :, :]))
                        link(dve.tensor_scalar(gates_r[:, :, :], gates_r[:, :, :], 0.5, None, ALU.mult))
                        link(dve.tensor_tensor(cw2[:, :], gates[:, 0, :], gates_r[:, 0, :], ALU.mult))

                    for c in range(SC):
                        shared_mul(c)
                        if c == 0:
                            for q in range(before_up, early):
                                if q not in by_pool:
                                    job_low(dve, q, s_wl)
                        if c == 1:
                            slots()
                            weights()
                        for q in late_of[c]:
                            if q not in by_pool:
                                job_low(dve, q, s_wl)
                        shared_low(c)
                    for j in range(NT // 2):
                        shared_out(j)

                    def tile_low(m, b):
                        dve.wait_ge(s_txh, m + 1)
                        dve.tensor_tensor(xeT_l[b][:, :], bank[b][:, 0:KD * P], xeT_h[b][:, :].bitcast(FP32),
                                          ALU.subtract).then_inc(s_txl, 1)

                    def inner_low(m, b):
                        dve.wait_ge(s_thh, m + 1)
                        dve.tensor_tensor(heT_l[b][:, :], bank[4 + b][0:IC, 0:2 * P], heT_h[b][:, :].bitcast(FP32),
                                          ALU.subtract).then_inc(s_thl, 1)

                    def inner_mul(m, b):
                        dve.wait_ge(s_es, m + 1)
                        dve.tensor_tensor(he[b][:, :], he[b][:, :], bank[2 + b][:, IM:2 * IM],
                                          ALU.mult).then_inc(s_em, 1)

                    tile_low(0, 0)
                    tile_low(1, 1)
                    inner_mul(0, 0)
                    with dve.Fori(0, (NM - 3) // 2) as i:
                        for b in range(2):
                            m = 2 * i + 1 + b
                            tile_low(m + 1, b)
                            inner_mul(m, 1 - b)
                            inner_low(m - 1, b)
                    m = NM - 2
                    tile_low(m + 1, 0)
                    inner_mul(m, 1)
                    inner_low(m - 1, 0)
                    inner_mul(m + 1, 0)
                    inner_low(m, 1)
                    inner_low(m + 1, 0)

                    def add(g):
                        j, t = divmod(g, TOP_K)
                        dve.wait_ge(s_gath[g % NT], 16 * (g // NT + 1 + (0 if first else TOP_K)))
                        if g:
                            dve.wait_ge(s_add, g)
                        w = gates_r[:, 0, j:j + 1] if t == 0 else cw2[:, j:j + 1]
                        dve.scalar_tensor_tensor(x_res[:, j, :], xn[:, g % NT, :], w, x_res[:, j, :],
                                                 ALU.mult, ALU.add).then_inc(s_add, 1)

                    dve.wait_ge(s_dnv, NT // 2)
                    g = 0
                    for c in range(SC, 2 * SC):
                        shared_mul(c)
                        shared_low(c)
                        for _ in range(2 if c >= SC + 2 else 0):
                            add(g)
                            g += 1
                    for j in range(NT // 2, NT):
                        shared_out(j)
                    dve.wait_ge(s_dnv, NT)
                    while g < TOP_K * NT:
                        add(g)
                        g += 1

                @block.tensor
                def _(pe):
                    if first:
                        pe.wait_ge(s_cst, 16)
                    norm_transposes(pe, n)
                    pe.wait_ge(n["xth"], 4)
                    pe.wait_ge(n["xtl"], 4)
                    if first:
                        pe.wait_ge(s_gh, 1)
                        pe.wait_ge(s_gl, 1)
                    for half in range(2):
                        toks = slice(half * HALF, (half + 1) * HALF)
                        for k in range(KD):
                            last = split_matmuls(pe, bank[5 + half][:, :], (wg_h[:, k, :], wg_l[:, k, :]),
                                                 (xT_h[:, k, toks], xT_l[:, k, toks]), k == 0, k == KD - 1)
                        last.then_inc(s_lgt, 1)
                    if first:
                        pe.wait_ge(s_wh, before_up)
                        wait_low(pe, before_up - 1)

                    def shared_up(c):
                        half, ch = divmod(c, SC)
                        if c >= 2:
                            pe.wait_ge(s_hm, c - 1)
                        toks = slice(half * HALF, (half + 1) * HALF)
                        for g in range(2):
                            cols = slice(g * ISP + ch * P, g * ISP + (ch + 1) * P)
                            for k in range(KD):
                                last = split_matmuls(pe, bank[2 * (c % 2) + g][:, :],
                                                     (wgu_h[:, k, cols], wgu_l[:, k, cols]),
                                                     (xT_h[:, k, toks], xT_l[:, k, toks]), k == 0, k == KD - 1)
                        last.then_inc(s_up, 1)

                    def shared_down(half):
                        pe.wait_ge(s_hh, SC * (half + 1))
                        pe.wait_ge(s_hl, SC * (half + 1))
                        for j in range(4 * half, 4 * half + 4):
                            if j % 4 >= 2:
                                pe.wait_ge(s_dnv, j - 1)
                            toks = slice((j % 4) * P, (j % 4 + 1) * P)
                            for c in range(SC):
                                last = split_matmuls(pe, bank[6 + j % 2][:, 0:D],
                                                     (hT_h[:, c, toks], hT_l[:, c, toks]),
                                                     (wd_h[:, c, :], wd_l[:, c, :]), c == 0, c == SC - 1)
                            last.then_inc(s_dn, 1)

                    shared_up(0)
                    pe.wait_ge(s_lgt_sb, 2)
                    for j in range(NT):
                        last = pe.transpose(bank[4][:, j * NG:(j + 1) * NG],
                                            lgT[j // 4][0:NG, (j % 4) * P:(j % 4 + 1) * P],
                                            cst[0:NG, C_ID:C_ID + NG])
                    last.then_inc(s_logits, 1)
                    shared_up(1)
                    if first:
                        pe.wait_ge(s_rw, 1)
                    pe.wait_ge(s_assigned, 1)
                    for a in range(2):
                        last = pe.matmul(bank[5][:, a * NT * NE:(a + 1) * NT * NE], rank_w[:, a, :], assigned[:, :],
                                         start=True, stop=True)
                    last.then_inc(s_rank, 1)
                    for c in range(2, SC):
                        shared_up(c)
                    if first:
                        wait_low(pe, early - 1)
                    shared_down(0)

                    def tile_in(m, q, b):
                        pe.wait_ge(s_xe[b], 16 * (q + 1))
                        for k in range(KD):
                            last = pe.transpose(bank[b][:, k * P:(k + 1) * P], xe[b][:, k * P:(k + 1) * P], ident)
                        last.then_inc(s_tx, 1)

                    def expert_of(m):
                        return pe.value_load(tile_e[0:1, bass.ds(m, 1)], min_val=0, max_val=NE - 1)

                    def up(m, b):
                        e = expert_of(m)
                        pe.wait_ge(s_txh, m + 1)
                        pe.wait_ge(s_txl, m + 1)
                        for k in range(KD):
                            part = slice(k * P, (k + 1) * P)
                            last = split_matmuls(pe, bank[2 + b][:, 0:2 * IM],
                                                 (xeT_h[b][:, part], xeT_l[b][:, part]),
                                                 (w1_h[:, e, k, :], w1_l[:, e, k, :]), k == 0, k == KD - 1)
                        last.then_inc(s_eu, 1)

                    def inner_turn(m, b):
                        pe.wait_ge(s_em, m + 1)
                        for c in range(2):
                            last = pe.transpose(bank[4 + b][0:IC, c * P:(c + 1) * P],
                                                he[b][:, c * IC:(c + 1) * IC], ident)
                        last.then_inc(s_th, 1)

                    def down(m, b, guard=True):
                        e = expert_of(m)
                        pe.wait_ge(s_thh, m + 1)
                        pe.wait_ge(s_thl, m + 1)
                        if guard:
                            pe.wait_ge(s_ye, m - 1)
                        for c in range(2):
                            part = slice(c * P, (c + 1) * P)
                            last = split_matmuls(pe, bank[6 + b][:, 0:D],
                                                 (heT_h[b][:, part], heT_l[b][:, part]),
                                                 (w2_h[:, e, c, :], w2_l[:, e, c, :]), c == 0, c == 1)
                        last.then_inc(s_ed, 1)

                    def step(m, q, b, guard=True):
                        tile_in(m + 1, q + b, 1 - b)
                        up(m, b)
                        inner_turn(m - 1, 1 - b)
                        down(m - 2, b, guard)

                    tile_in(0, 0, 0)
                    tile_in(1, 0, 1)
                    pe.wait_ge(s_wh, len(jobs))
                    wait_low(pe, len(jobs) - 1)
                    pe.wait_ge(s_expert, 1)
                    pe.wait_ge(s_dnv, NT // 2)
                    up(0, 0)
                    tile_in(2, 1, 0)
                    up(1, 1)
                    inner_turn(0, 0)
                    step(2, 1, 0, False)
                    step(3, 1, 1, False)
                    with pe.Fori(2, NM // 2) as i:
                        step(2 * i, i, 0)
                        step(2 * i + 1, i, 1)
                    m = NM - 1
                    up(m, 0)
                    inner_turn(m - 1, 1)
                    down(m - 2, 0)
                    inner_turn(m, 0)
                    down(m - 1, 1)
                    down(m, 0)
                    for c in range(SC, 2 * SC):
                        shared_up(c)
                    pe.wait_ge(s_ye, NM)
                    shared_down(1)

                block_ctx.close()

        def attention():
            loc = ExitStack()
            with loc:
                def sb(name, shape, dt=FP32):
                    return sbuf(f"{name}_a", shape, dt, loc)

                QKV = 3 * KD * 2 * DH
                w_raw = sb("w_raw", [P, QKV])
                w_h = sb("w_h", [P, 3, KD, 2 * DH], FP32R)
                w_l = sb("w_l", [P, 3, KD, 2 * DH], FP32R)
                wo_raw = sb("wo_raw", [P, 2 * D])
                wo_h = sb("wo_h", [P, 2, D], FP32R)
                wo_l = sb("wo_l", [P, 2, D], FP32R)
                qk = sb("qk", [P, 2, 2, TOK])
                v = sb("v", [P, NT, 2 * DH])
                bias_all = sb("bias_all", [P, 3, NH])
                bias = sb("bias", [P, 3, 2])
                bo_sb = sb("bo_sb", [P, D])
                NS = 4
                s = [sb(f"s{b}", [P, 3 * P]) for b in range(NS)]
                mn = sb("mn", [P, NS, 2])
                rs = sb("rs", [P, NS, 2])
                rr = sb("rr", [P, NS, 2])
                pT = [sb(f"pT{b}", [P, 3 * P]) for b in range(2)]
                zT_h = sb("zT_h", [P, 2, TOK], FP32R)
                zT_l = sb("zT_l", [P, 2, TOK], FP32R)

                n = norm_sems("a")
                s_b = sem("a_bias")
                s_bo = sem("a_bo")
                s_bp = sem("a_bias_pair")
                s_wraw = sem("a_wraw")
                s_woraw = sem("a_woraw")
                s_wh = sem("a_wh")
                s_wl = sem("a_wl")
                s_woh = sem("a_woh")
                s_wol = sem("a_wol")
                s_proj = sem("a_proj")
                s_pa = sem("a_proj_act")
                s_pv = sem("a_proj_dve")
                s_sc = sem("a_scores")
                s_sm = sem("a_masked")
                s_mn = sem("a_min")
                s_e = sem("a_exp")
                s_rr = sem("a_recip")
                s_p = sem("a_probs")
                s_pt = sem("a_pT_psum")
                s_ptv = sem("a_pT")
                s_z = sem("a_z_psum")
                s_zh = sem("a_zh")
                s_zl = sem("a_zl")
                s_o = sem("a_o_psum")
                s_ov = sem("a_o_added")
                U = 2 * BATCH
                PROJ = 12
                ORDER = [("p", 0), ("p", 1), ("o", 3)] + [("p", g) for g in range(2, PROJ)] + \
                        [("o", 0), ("o", 1), ("o", 2)]
                RING = 3
                BANK = {item: at % RING for at, item in enumerate(ORDER)}

                def unit(u):
                    return u // 2, u % 2

                block_ctx = ExitStack()
                block = block_ctx.enter_context(nc.Block())

                @block.sync
                def _(sp):
                    sp.dma_start(w_raw[:, :], wqkv[0]).then_inc(s_wraw, 16)
                    sp.dma_start(wo_raw[:, :], wo[0]).then_inc(s_woraw, 16)
                    sp.dma_start(bias_all[:, :, :], bqkv).then_inc(s_b, 16)
                    sp.dma_start(bo_sb[:, :], bo.partition_broadcast(P)).then_inc(s_bo, 16)
                    with sp.Fori(1, NP) as i:
                        sp.wait_ge(s_wl, i)
                        sp.dma_start(w_raw[:, :], wqkv[i]).then_inc(s_wraw, 16)
                        sp.wait_ge(s_wol, i)
                        sp.dma_start(wo_raw[:, :], wo[i]).then_inc(s_woraw, 16)

                PIECE = QKV // 6
                zero = cst[:, C_ZERO:C_ZERO + 1]

                @block.gpsimd
                def _(pool):
                    def w_flat(t):
                        return t[:, :, :, :].rearrange("p a b c -> p (a b c)")

                    def o_flat(t):
                        return t[:, :, :].rearrange("p a b -> p (a b)")

                    def split_qkv(i, c):
                        pair = 0 if i is first_pair else i
                        if c == 0:
                            pool.wait_ge(s_wraw, 16 * (pair + 1))
                        if i is not first_pair:
                            pool.wait_ge(s_proj, PROJ * (i - 1) + 4 * (c // 2 + 1))
                        cols = slice(c * PIECE, (c + 1) * PIECE)
                        pool.tensor_tensor(w_flat(w_h)[:, cols], w_raw[:, cols], zero.to_broadcast([P, PIECE]),
                                           ALU.add).then_inc(s_wh, 1)
                        pool.wait_ge(s_wh, 6 * pair + c + 1)
                        ins = pool.tensor_tensor(w_flat(w_l)[:, cols], w_raw[:, cols],
                                                 w_flat(w_h)[:, cols].bitcast(FP32), ALU.subtract)
                        if c == 5:
                            ins.then_inc(s_wl, 1)

                    first_pair = "first"

                    norm_rstd(pool, n)
                    for c in range(6):
                        split_qkv(first_pair, c)

                    def body(i, more):
                        pool.wait_ge(s_woraw, 16 * (i + 1))
                        if more != "first":
                            pool.wait_ge(s_o, BATCH * i)
                        pool.tensor_tensor(o_flat(wo_h), wo_raw[:, :], zero.to_broadcast([P, 2 * D]),
                                           ALU.add).then_inc(s_woh, 1)
                        pool.wait_ge(s_woh, i + 1)
                        pool.tensor_tensor(o_flat(wo_l), wo_raw[:, :], o_flat(wo_h).bitcast(FP32),
                                           ALU.subtract).then_inc(s_wol, 1)
                        if more != "last":
                            for c in range(4):
                                split_qkv(i + 1, c)
                        for u in range(U):
                            pool.wait_ge(s_rr, U * i + u + 1)
                            b = u % NS
                            pool.tensor_tensor(s[b][:, 0:P], s[b][:, 0:P],
                                               rr[:, b, 0:1].to_broadcast([P, P]), ALU.mult).then_inc(s_p, 1)
                            pool.tensor_tensor(s[b][:, P:3 * P], s[b][:, P:3 * P],
                                               rr[:, b, 1:2].to_broadcast([P, 2 * P]), ALU.mult).then_inc(s_p, 1)
                            if more != "last" and u in (3, 5):
                                split_qkv(i + 1, 4 + (u - 3) // 2)

                    body(0, "first")
                    with pool.Fori(1, NP - 1) as i:
                        body(i, "more")
                    body(NP - 1, "last")

                def proj_out(g, t):
                    if g < 8:
                        return qk[:, g // 4, (g // 2) % 2, (g % 2) * HALF:(g % 2 + 1) * HALF]
                    return v[:, 2 * (g - 8):2 * (g - 8) + 2, :].rearrange("p a b -> p (a b)")

                @block.scalar
                def _(act):
                    norm_split_high(act, n)

                    def proj(i, g):
                        act.wait_ge(s_proj, PROJ * i + g + 1)
                        b = BANK["p", g]
                        if g < 8:
                            act.activation(proj_out(g, None), bank[b][:, :], ACT.Identity,
                                           bias=bias[:, g // 4, (g // 2) % 2:(g // 2) % 2 + 1]).then_inc(s_pa, 1)
                        else:
                            act.activation(proj_out(g, None), bank[b][:, :], ACT.Copy).then_inc(s_pa, 1)

                    def exps(i, u):
                        b = u % NS
                        act.wait_ge(s_mn, 2 * (U * i + u + 1))
                        for t, cols in ((0, slice(0, P)), (1, slice(P, 3 * P))):
                            act.activation(s[b][:, cols], s[b][:, cols], ACT.Exp, bias=mn[:, b, t:t + 1], scale=-1.0,
                                           accum_out=rs[:, b, t:t + 1]).then_inc(s_e, 1)

                    def turned(i, u):
                        act.wait_ge(s_pt, U * i + u + 1)
                        act.activation(pT[u % 2][:, :], bank[5 + u % 2][:, 0:3 * P], ACT.Copy).then_inc(s_ptv, 1)

                    def z_high(i, u):
                        bt, h = unit(u)
                        act.wait_ge(s_z, U * i + u + 1)
                        act.activation(zT_h[:, h, bt * SEQ:(bt + 1) * SEQ], bank[7][:, 0:SEQ], ACT.Identity,
                                       bias=bias[:, 2, h:h + 1]).then_inc(s_zh, 1)

                    with act.Fori(0, NP) as i:
                        act.wait_ge(s_bp, i + 1)
                        for g in (0, 2, 4, 6, 8):
                            proj(i, g)
                        exps(i, 0)
                        proj(i, 10)
                        exps(i, 1)
                        for u in range(U):
                            turned(i, u)
                            if u + 2 < U:
                                exps(i, u + 2)
                            z_high(i, u)

                @block.vector
                def _(dve):
                    norm_stats(dve, n, None)
                    norm_apply(dve, n)
                    norm_split_low(dve, n)
                    dve.wait_ge(s_b, 16)
                    dve.wait_ge(s_bo, 16)
                    dve.wait_ge(n["xn"], NT)
                    for j in range(NT):
                        last = dve.tensor_tensor(x_res[:, j, :], x_res[:, j, :], bo_sb[:, :], ALU.add)
                    last.then_inc(s_bo, 1)
                    dve.tensor_copy(bias[:, :, :], bias_all[:, :, 0:2]).then_inc(s_bp, 1)
                    dve.wait_ge(s_bo, 17)

                    def proj(i, g):
                        dve.wait_ge(s_proj, PROJ * i + g + 1)
                        b = BANK["p", g]
                        if g < 8:
                            dve.tensor_scalar(proj_out(g, None), bank[b][:, :],
                                              bias[:, g // 4, (g // 2) % 2:(g // 2) % 2 + 1], None,
                                              ALU.add).then_inc(s_pv, 1)
                        else:
                            dve.tensor_copy(proj_out(g, None), bank[b][:, :]).then_inc(s_pv, 1)

                    def masked(i, u):
                        b = u % NS
                        at = U * i + u
                        dve.wait_ge(s_sc, at + 1)
                        dve.scalar_tensor_tensor(s[b][:, :], bank[3 + u % 2][:, 0:3 * P], -INV_SCALE,
                                                 cst[:, C_MASK:C_MASK + 3 * P], ALU.mult, ALU.max).then_inc(s_sm, 1)
                        dve.wait_ge(s_sm, at + 1)
                        for t, cols in ((0, slice(0, P)), (1, slice(P, 3 * P))):
                            dve.tensor_reduce(mn[:, b, t:t + 1], s[b][:, cols], op=ALU.min,
                                              axis=AX.X).then_inc(s_mn, 1)

                    def recip(i, u):
                        b = u % NS
                        dve.wait_ge(s_e, 2 * (U * i + u + 1))
                        dve.reciprocal(rr[:, b, :], rs[:, b, :]).then_inc(s_rr, 1)

                    def z_low(i, u):
                        bt, h = unit(u)
                        cols = slice(bt * SEQ, (bt + 1) * SEQ)
                        dve.wait_ge(s_zh, U * i + u + 1)
                        dve.scalar_tensor_tensor(zT_l[:, h, cols], bank[7][:, 0:SEQ],
                                                 bias[:, 2, h:h + 1], zT_h[:, h, cols].bitcast(FP32),
                                                 ALU.add, ALU.subtract).then_inc(s_zl, 1)

                    def added(i, bt):
                        dve.wait_ge(s_o, BATCH * i + bt + 1)
                        r = x_res[:, 2 * bt:2 * bt + 2, :].rearrange("p a b -> p (a b)")
                        dve.tensor_tensor(r, r, bank[BANK["o", bt]][:, :], ALU.add).then_inc(s_ov, 1)

                    def body(i, fresh=False):
                        dve.wait_ge(s_bp, i + 1)
                        proj(i, 1)
                        if not fresh:
                            added(i - 1, BATCH - 1)
                        for g in (3, 5, 7):
                            proj(i, g)
                        masked(i, 0)
                        proj(i, 9)
                        masked(i, 1)
                        recip(i, 0)
                        masked(i, 2)
                        proj(i, 11)
                        recip(i, 1)
                        for u in range(U):
                            if u + 3 < U:
                                masked(i, u + 3)
                            if u + 2 < U:
                                recip(i, u + 2)
                            z_low(i, u)
                            if u == U - 1:
                                dve.wait_ge(s_zl, U * (i + 1))
                            if u >= 5:
                                added(i, u - 5)

                    def next_bias(i):
                        dve.tensor_copy(bias[:, :, :], bias_all[:, :, bass.ds(2 * i + 2, 2)]).then_inc(s_bp, 1)

                    body(0, True)
                    next_bias(0)
                    with dve.Fori(1, NP - 1) as i:
                        body(i)
                        next_bias(i)
                    body(NP - 1)
                    added(NP - 1, BATCH - 1)

                @block.tensor
                def _(pe):
                    norm_transposes(pe, n)
                    pe.wait_ge(n["xth"], 4)
                    pe.wait_ge(n["xtl"], 4)

                    def bank_free(i, item, fresh):
                        at = ORDER.index(item)
                        back = next(d for d in range(1, len(ORDER) + 1) if BANK[ORDER[at - d]] == BANK[item])
                        kind, x = ORDER[at - back]
                        pair = i if at >= back else i - 1
                        if fresh and (at < back or (kind, x) == ("o", 3)):
                            return
                        if kind == "o":
                            pe.wait_ge(s_ov, BATCH * pair + (x + 1) % BATCH)
                        elif x % 2 == 0:
                            pe.wait_ge(s_pa, (PROJ // 2) * pair + x // 2 + 1)
                        else:
                            pe.wait_ge(s_pv, (PROJ // 2) * pair + x // 2 + 1)

                    def proj(i, g, fresh):
                        b = BANK["p", g]
                        bank_free(i, ("p", g), fresh)
                        for k in range(KD):
                            if g < 8:
                                t, h, half = g // 4, (g // 2) % 2, g % 2
                                toks = slice(half * HALF, (half + 1) * HALF)
                                w = slice(h * DH, (h + 1) * DH)
                                last = split_matmuls(pe, bank[b][:, :], (w_h[:, t, k, w], w_l[:, t, k, w]),
                                                     (xT_h[:, k, toks], xT_l[:, k, toks]), k == 0, k == KD - 1)
                        if g >= 8:
                            for j in range(2):
                                toks = slice((2 * (g - 8) + j) * P, (2 * (g - 8) + j + 1) * P)
                                for k in range(KD):
                                    last = split_matmuls(pe, bank[b][:, j * 2 * DH:(j + 1) * 2 * DH],
                                                         (xT_h[:, k, toks], xT_l[:, k, toks]),
                                                         (w_h[:, 2, k, :], w_l[:, 2, k, :]), k == 0, k == KD - 1)
                        last.then_inc(s_proj, 1)

                    def scores(i, u):
                        bt, h = unit(u)
                        b = bank[3 + u % 2]
                        if u == 0:
                            pe.wait_ge(s_pa, (PROJ // 2) * i + 4)
                            pe.wait_ge(s_pv, (PROJ // 2) * i + 4)
                        if u >= 2:
                            pe.wait_ge(s_sm, U * i + u - 1)
                        q, k = qk[:, 0, h, :], qk[:, 1, h, :]
                        t0 = bt * SEQ
                        pe.matmul(b[:, 0:P], q[:, t0:t0 + P], k[:, t0:t0 + P], start=True, stop=True)
                        pe.matmul(b[:, P:3 * P], q[:, t0 + P:t0 + 2 * P], k[:, t0:t0 + 2 * P],
                                  start=True, stop=True).then_inc(s_sc, 1)

                    def turn(i, u):
                        pe.wait_ge(s_p, 2 * (U * i + u + 1))
                        if u >= 2:
                            pe.wait_ge(s_ptv, U * i + u - 1)
                        for c in range(3):
                            last = pe.transpose(bank[5 + u % 2][:, c * P:(c + 1) * P],
                                                s[u % NS][:, c * P:(c + 1) * P], ident)
                        last.then_inc(s_pt, 1)

                    def mix(i, u):
                        bt, h = unit(u)
                        pe.wait_ge(s_ptv, U * i + u + 1)
                        if u == 0:
                            pe.wait_ge(s_pa, (PROJ // 2) * (i + 1))
                            pe.wait_ge(s_pv, (PROJ // 2) * (i + 1))
                        if u >= 1:
                            pe.wait_ge(s_zl, U * i + u)
                        e = slice(h * DH, (h + 1) * DH)
                        pe.matmul(bank[7][:, 0:2 * P], v[:, 2 * bt, e], pT[u % 2][:, 0:2 * P], start=True, stop=False)
                        pe.matmul(bank[7][:, P:2 * P], v[:, 2 * bt + 1, e], pT[u % 2][:, 2 * P:3 * P],
                                  start=False, stop=True).then_inc(s_z, 1)

                    def project(i, bt, fresh=False):
                        pe.wait_ge(s_zh, U * i + 2 * bt + 2)
                        pe.wait_ge(s_zl, U * i + 2 * bt + 2)
                        if bt == 0:
                            pe.wait_ge(s_wol, i + 1)
                        bank_free(i + (bt == BATCH - 1), ("o", bt), fresh)
                        for j in range(2):
                            toks = slice((2 * bt + j) * P, (2 * bt + j + 1) * P)
                            for h in range(2):
                                last = split_matmuls(pe, bank[BANK["o", bt]][:, j * D:(j + 1) * D],
                                                     (zT_h[:, h, toks], zT_l[:, h, toks]),
                                                     (wo_h[:, h, :], wo_l[:, h, :]), h == 0, h == 1)
                        last.then_inc(s_o, 1)

                    def body(i, fresh):
                        pe.wait_ge(s_wl, i + 1)
                        proj(i, 0, fresh)
                        proj(i, 1, fresh)
                        if not fresh:
                            project(i - 1, BATCH - 1)
                        for g in range(2, 9):
                            proj(i, g, fresh)
                        scores(i, 0)
                        proj(i, 9, fresh)
                        scores(i, 1)
                        proj(i, 10, fresh)
                        scores(i, 2)
                        proj(i, 11, fresh)
                        for u in range(U):
                            turn(i, u)
                            if u + 3 < U:
                                scores(i, u + 3)
                            if u >= 5:
                                project(i, u - 5)
                            mix(i, u)

                    body(0, True)
                    with pe.Fori(1, NP) as i:
                        body(i, False)
                    project(NP - 1, BATCH - 1)

                block_ctx.close()

        ffn("f0", True)
        attention()
        ffn("f1", False)


def kernel(**inputs):
    import concourse.bacc as bacc
    from concourse.bass_utils import run_bass_kernel_spmd

    def chunks(w, rows, p):
        w = w.reshape(*w.shape[:-2], rows // p, p, w.shape[-1])
        return np.moveaxis(w, -2, 0)

    a = {k.removeprefix("L0_"): np.asarray(v) for k, v in inputs.items()}
    gu = a["ffn_shared_gate_up_w"].reshape(2, ISH, D)
    gu = np.concatenate([gu, np.zeros((2, ISP - ISH, D), np.float32)], 1).reshape(2 * ISP, D)
    dn = np.concatenate([a["ffn_shared_down_w"], np.zeros((D, ISP - ISH), np.float32)], 1)
    gate = np.concatenate([a["ffn_gate_w"], a["ffn_shared_gate_w"], np.zeros((P - NG, D), np.float32)], 0)

    def heads(w):
        w = w.reshape(NP, 2, KD, P, DH)
        return w.transpose(0, 3, 2, 1, 4)

    arrays = {
        "x_in": a["attn_x"].reshape(TOK, D),
        "consts": constants(),
        "wgate": chunks(gate.T, D, P).reshape(P, KD * P),
        "wgu": chunks(gu.T, D, P),
        "wd": chunks(dn.T, ISP, P),
        "w1": chunks(a["ffn_w1"].transpose(0, 2, 1), D, P),
        "w2": chunks(a["ffn_w2"].transpose(0, 2, 1), IM, IC),
        "wqkv": np.stack([heads(a[f"attn_W_{t}"]) for t in "QKV"], 2).reshape(NP, P, -1),
        "wo": a["attn_W_O"].reshape(NP, 2, DH, D).transpose(0, 2, 1, 3).reshape(NP, P, 2 * D),
        "bqkv": np.stack([a[f"attn_b_{t}"].T for t in "QKV"], 1),
        "bo": a["attn_b_O"],
    }
    nc = bacc.Bacc("TRN2", target_bir_lowering=False, num_devices=1)
    ins, aps = {}, {}
    for name, arr in arrays.items():
        arr = np.ascontiguousarray(arr)
        ins[f"in_{name}"] = arr
        aps[name] = nc.dram_tensor(f"in_{name}", arr.shape, mybir.dt.from_np(arr.dtype), kind="ExternalInput").ap()
    aps["out"] = nc.dram_tensor("out_0", (TOK, D), FP32, kind="ExternalOutput").ap()
    macaron(nc, **aps)
    r = run_bass_kernel_spmd(nc, [ins], core_ids=[0])
    return r.results[0]["out_0"].reshape(BATCH, SEQ, D)
```

```python
import numpy as np
import concourse.bass as bass
from concourse import mybir
from contextlib import ExitStack

FP32 = mybir.dt.float32
FP32R = mybir.dt.float32r
BF16 = mybir.dt.bfloat16
I32 = mybir.dt.int32
ALU = mybir.AluOpType
ACT = mybir.ActivationFunctionType
AX = mybir.AxisListType

P = 128
BATCH, SEQ, D = 4, 256, 256
TOK = BATCH * SEQ
NT = TOK // P
KD = D // P
HALF = 512
NE = 8
TOP_K = 2
IM = 176
IC = IM // 2
ISH = 704
SC = -(-ISH // P)
LASTW = ISH - (SC - 1) * P
assert 2 * LASTW == P
CH = 2 * KD * P
WGU = 2 * KD * ISH
STW = 3 * D
NG = NE + 1
NH, DH = 16, 128
NP = NH // 2
NM = TOP_K * NT + NE - 1
VOID = -(-NM // NT) * NT
AHEAD = 2
INV_AT = 5
ADDS = (0, 0, 0, 1, 1, 1)
WARM = (24, 7, 8, 16, 8, 14)
STEPS = 6
OUT_LAG = 6
NST = 4
EPS = 1e-5
IGNORE = -100000.0
BIG = 3.0e38
INV_SCALE = 1.0 / float(np.sqrt(np.float32(DH)))

POOL_JOBS_FIRST = (1, 4, 5, 6, 7, 8, 9, 10, 11)
POOL_JOBS_SECOND = (0, 1, 2, 3, 4, 5)
POOL_LATE = (13, 15, 17, 19)
CUTS_FIRST = (3, 4, 6, 8, 10, 12, 19, 23)
CUTS_SECOND = (0, 1, 2, 4, 5, 6, 7, 8)
XN_OUT = (1, 3)

R1 = 8

C_ID = 0
C_DESC = C_ID + P
C_M128 = C_DESC + NE
C_LT = C_M128 + NT
C_MI = C_LT + NE * NE
C_MP = C_MI + NM
C_P = C_MP + NM
C_J = C_P + 1
C_VOID = C_J + TOP_K * NT
C_EPS = C_VOID + NM
C_NH = C_EPS + NT
C_ZERO = C_NH + NT
C_U = C_ZERO + 1
C_ONE = C_U + P
C_COL = C_ONE + P
C_MASK = C_COL + P
C_N = C_MASK + 3 * P


def constants():
    c = np.zeros((P, C_N), np.float32)
    r = np.arange(P)
    c[:, C_ID:C_ID + P] = np.eye(P)
    c[:, C_U:C_U + P] = r[:, None] < r[None, :]
    c[:, C_ONE:C_ONE + P] = 1.0
    diagonal = np.where(r[None, :] <= r[:, None], -BIG, -IGNORE)
    c[:, C_MASK:C_MASK + P] = diagonal
    c[:, C_MASK + P:C_MASK + 2 * P] = -BIG
    c[:, C_MASK + 2 * P:C_MASK + 3 * P] = diagonal
    c[:, C_DESC:C_DESC + NE] = NE - np.arange(NE)
    c[:, C_M128:C_M128 + NT] = P * np.arange(NT)
    e = np.arange(NE)
    c[:, C_LT:C_LT + NE * NE] = (e[None, :] < e[:, None]).reshape(-1)
    c[:, C_MI:C_MI + NM] = np.arange(NM)
    c[:, C_MP:C_MP + NM] = P * np.arange(NM)
    c[:, C_P] = r
    c[:, C_J:C_J + TOP_K * NT] = VOID + np.arange(TOP_K * NT)
    c[:, C_VOID:C_VOID + NM] = P * np.arange(NM) + r[:, None]
    c[:, C_COL:C_COL + P] = r
    c[:, C_EPS:C_EPS + NT] = EPS
    c[:, C_NH:C_NH + NT] = -0.5
    return c


def macaron(nc, x_in, consts, wgate, wgu, wd, w1, w2, wqkv, wo, bqkv, bo, out):
    ctx = ExitStack()
    with ctx:
        def sbuf(name, shape, dt=FP32, stack=ctx):
            return stack.enter_context(nc.sbuf_tensor(name, shape, dt))

        def sem(name):
            return ctx.enter_context(nc.semaphore(name))

        xd = nc.dram_tensor("x_normed", (TOK, D), FP32, kind="Internal").ap()
        yd = nc.dram_tensor("y_by_token", (VOID * P + TOP_K * TOK, D), FP32, kind="Internal").ap()

        cst = sbuf("cst", [P, C_N])
        x_res = sbuf("x_res", [P, NT, D])
        xn = sbuf("xn", [P, NT, D])
        xT_h = sbuf("xT_h", [P, KD, TOK], FP32R)
        xT_l = sbuf("xT_l", [P, KD, TOK], FP32R)
        wg_h = sbuf("wg_h", [P, KD, P], FP32R)
        wg_l = sbuf("wg_l", [P, KD, P], FP32R)
        wgu_h = sbuf("wgu_h", [P, WGU], FP32R)
        wgu_l = sbuf("wgu_l", [P, WGU], FP32R)
        wd_h = sbuf("wd_h", [P, SC, D], FP32R)
        wd_l = sbuf("wd_l", [P, SC, D], FP32R)
        w1_h = sbuf("w1_h", [P, NE, KD, 2 * IM], FP32R)
        w1_l = sbuf("w1_l", [P, NE, KD, 2 * IM], FP32R)
        rank_w = sbuf("rank_w", [P, 2, P], BF16)
        stats = sbuf("stats", [P, NT, 6])
        mv = sbuf("mv", [P, NT, 2])
        rstd = sbuf("rstd", [P, NT])
        bank = [ctx.enter_context(nc.psum_tensor(f"bank{b}", [P, HALF], FP32)) for b in range(8)]
        ident = cst[:, C_ID:C_ID + P]
        Y_BUF = (2, 3, 0, 1, 4, 5, 2, 3)
        s_y = [sem(f"s_y{b}") for b in range(6)]
        y_in = [0] * 6

        QKV = 3 * KD * 2 * DH
        area = sbuf("area", [P, NST * STW])
        area_h = sbuf("area_h", [P, 2 * NE * D], FP32R)
        area_l = sbuf("area_l", [P, 2 * NE * D], FP32R)
        assert QKV + 2 * D <= NST * STW and QKV + 2 * TOK + 2 * D <= 2 * NE * D
        w_raw, wo_raw = area[:, 0:QKV], area[:, QKV:QKV + 2 * D]
        bias_all = sbuf("bias_all", [P, 3, NH])
        s_b = sem("a_bias")
        s_wraw = sem("a_wraw")
        s_woraw = sem("a_woraw")
        s_qh = sem("a_wh")
        s_ql = sem("a_wl")

        def attn_w(t, kind):
            if kind == "w":
                return t[:, 0:QKV].rearrange("p (t k e) -> p t k e", t=3, k=KD)
            if kind == "z":
                return t[:, QKV:QKV + 2 * TOK].rearrange("p (h n) -> p h n", h=2)
            return t[:, QKV + 2 * TOK:QKV + 2 * TOK + 2 * D].rearrange("p (h n) -> p h n", h=2)

        def split_matmuls(pe, psum, lhs, rhs, first, last):
            pe.matmul(psum, lhs[0], rhs[0], start=first, stop=False)
            pe.matmul(psum, lhs[0], rhs[1], start=False, stop=False)
            return pe.matmul(psum, lhs[1], rhs[0], start=False, stop=last)

        def keep_warm(pe, b, count):
            for _ in range(count):
                pe.matmul(bank[b][:, 0:2 * P], rank_w[:, 0, :], rank_w[:, :, :].rearrange("p a b -> p (a b)"),
                          start=True, stop=True)

        HT = NT // 2

        def norm_sems(tag):
            return {n: sem(f"{n}_{tag}") for n in ("stats", "mv", "rstd", "xn", "xt", "xth", "xtl")}

        def norm_stats(dve, s, half, loaded=None):
            for j in range(half * HT, (half + 1) * HT):
                if loaded is not None:
                    dve.wait_ge(loaded[j // 2], 16)
                dve.bn_stats(stats[:, j, :], x_res[:, j, :]).then_inc(s["stats"], 1)
            for j in range(half * HT, (half + 1) * HT):
                dve.wait_ge(s["stats"], j + 1)
                dve.bn_aggr(mv[:, j, :], stats[:, j, :]).then_inc(s["mv"], 1)

        def norm_rstd(pool, s, half):
            js = slice(half * HT, (half + 1) * HT)
            pool.wait_ge(s["mv"], (half + 1) * HT)
            pool.tensor_tensor(rstd[:, js], mv[:, js, 1], cst[:, C_EPS:C_EPS + HT], ALU.add).then_inc(s["rstd"], 1)
            pool.wait_ge(s["rstd"], 2 * half + 1)
            pool.tensor_tensor(rstd[:, js], rstd[:, js], cst[:, C_NH:C_NH + HT], ALU.pow).then_inc(s["rstd"], 1)

        def norm_apply(dve, s, half):
            dve.wait_ge(s["rstd"], 2 * half + 2)
            for j in range(half * HT, (half + 1) * HT):
                dve.tensor_scalar(xn[:, j, :], x_res[:, j, :], mv[:, j, 0:1], rstd[:, j:j + 1],
                                  ALU.subtract, ALU.mult).then_inc(s["xn"], 1)

        def norm_turn(pe, s, half, banks):
            pe.wait_ge(s["xn"], (half + 1) * HT)
            for k in range(KD):
                for j in range(HT):
                    last = pe.transpose(bank[banks[k]][:, j * P:(j + 1) * P],
                                        xn[:, half * HT + j, k * P:(k + 1) * P], ident)
                last.then_inc(s["xt"], 1)

        def norm_high(act, s, half, banks):
            for k in range(KD):
                act.wait_ge(s["xt"], KD * half + k + 1)
                act.activation(xT_h[:, k, half * HALF:(half + 1) * HALF], bank[banks[k]][:, :],
                               ACT.Copy).then_inc(s["xth"], 1)

        def norm_low(dve, s, half, banks):
            cols = slice(half * HALF, (half + 1) * HALF)
            for k in range(KD):
                dve.wait_ge(s["xth"], KD * half + k + 1)
                dve.tensor_tensor(xT_l[:, k, cols], bank[banks[k]][:, :], xT_h[:, k, cols].bitcast(FP32),
                                  ALU.subtract).then_inc(s["xtl"], 1)

        def norm_wait(pe, s, half):
            pe.wait_ge(s["xth"], KD * (half + 1))
            pe.wait_ge(s["xtl"], KD * (half + 1))

        norm1, norm2, norm3 = norm_sems("norm1"), norm_sems("norm2"), norm_sems("norm3")

        def ffn(tag, first, n, after):
            loc = ExitStack()
            with loc:
                def sb(name, shape, dt=FP32):
                    return sbuf(f"{name}_{tag}", shape, dt, loc)

                w2_h = area_h[0:IC, :].rearrange("p (e c d) -> p e c d", e=NE, c=2)
                w2_l = area_l[0:IC, :].rearrange("p (e c d) -> p e c d", e=NE, c=2)
                stage = [area[:, b * STW:(b + 1) * STW] for b in range(NST)]
                wg_tile = sb("wg_tile", [P, max(KD * P, TOP_K * NT * NM)])
                wg_raw = wg_tile[:, 0:KD * P]
                tile_hot = wg_tile[:, 0:TOP_K * NT * NM].rearrange("p (a b) -> p a b", b=NM)
                hs = [sb(f"hs{b}", [P, HALF]) for b in range(2)]
                hT_h = sb("hT_h", [P, SC, HALF], FP32R)
                hT_l = sb("hT_l", [P, SC, HALF], FP32R)
                rows = sb("rows", [P, 4, D])
                xe, ye = [[rows[:, a + b, :] for b in range(2)] for a in (0, 2)]
                lgT = xe + ye
                xeT_h = [sb(f"xeT_h{b}", [P, KD * P], FP32R) for b in range(2)]
                xeT_l = [sb(f"xeT_l{b}", [P, KD * P], FP32R) for b in range(2)]
                row_hot = rows[:, :, :].rearrange("p a b -> p (a b)").bitcast(BF16).rearrange("p (a b) -> p a b", b=P)
                assert row_hot.shape[1] == TOK // P * TOP_K
                token_hot = sb("token_hot", [P, TOP_K * NT, 2, NM], BF16)
                slot_row = sb("slot_row", [P, TOP_K * NT], I32)
                slot_tile = sb("slot_tile", [P, TOP_K * NT], I32)
                place = sb("place", [P, NM], I32)
                tok_i = sb("tok_i", [P, NM], I32)
                he = [sb(f"he{b}", [P, IM]) for b in range(2)]
                heT_h = [sb(f"heT_h{b}", [IC, 2 * P], FP32R) for b in range(2)]
                heT_l = [sb(f"heT_l{b}", [IC, 2 * P], FP32R) for b in range(2)]
                lg = sb("lg", [P, NT, NG])
                dl = sb("dl", [P, NT, NE])
                sc = sb("sc", [P, NT, NE])
                sel = sb("sel", [P, TOP_K, NT, NE])
                tok_f = sel[:, :, :, :].rearrange("p t a b -> p (t a b)")[:, 0:NM]
                assigned = sb("assigned", [P, NT + 1, NE], BF16)
                best = sb("best", [P, NT])
                best2 = sb("best2", [P, NT])
                lead = sb("lead", [P, NT])
                cmp = sc
                assert NT == NE
                tiles_of = sb("tiles_of", [P, NE])
                base = sb("base", [P, NE])
                end = sb("end", [P, NE])
                slot = dl
                slot_f = sb("slot_f", [P, TOP_K * NT])
                slot_i = sb("slot_i", [P, TOP_K * NT], I32)
                tile_cmp = wg_tile[0:1, 0:NM * NE].rearrange("p (a b) -> p a b", b=NE)
                tile_f = sb("tile_f", [1, NM])
                tile_e = sb("tile_e", [1, NM], I32)
                gates = sb("gates", [P, 2, NT])
                gates_r = sb("gates_r", [P, 2, NT])
                cw2 = sb("cw2", [P, NT])

                if first:
                    s_x = [sem(f"s_x{j}") for j in range(0, NT, 2)]
                    s_cst, s_cst2, s_zero = sem("s_cst"), sem("s_cst_later"), sem("s_zero")
                    s_gate_in, s_gh, s_gl = sem("s_gate_in"), sem("s_gate_high"), sem("s_gate_low")
                s_stage = [sem(f"s_stage{b}_{tag}") for b in range(NST)]
                s_wh = sem(f"s_wh_{tag}")
                s_wl = sem(f"s_wl_{tag}")
                s_wlp = sem(f"s_wlp_{tag}")
                s_lgt = sem(f"s_lgt_{tag}")
                s_lgt_sb = sem(f"s_lgt_sb_{tag}")
                s_logits = sem(f"s_logits_{tag}")
                s_rw = sem(f"s_rw_{tag}")
                s_route = sem(f"s_route_{tag}")
                s_exp = sem(f"s_exp_{tag}")
                s_assigned = sem(f"s_assigned_{tag}")
                s_rank = sem(f"s_rank_{tag}")
                s_slot = sem(f"s_slot_{tag}")
                s_expert = sem(f"s_expert_{tag}")
                s_xd = sem(f"s_xd_{tag}")
                s_hot = sem(f"s_hot_{tag}")
                s_inv = sem(f"s_inv_{tag}")
                s_tok = sem(f"s_tok_{tag}")
                s_up = sem(f"s_up_{tag}")
                s_silu = sem(f"s_silu_{tag}")
                s_hm = sem(f"s_hm_{tag}")
                s_hh = sem(f"s_hh_{tag}")
                s_hl = sem(f"s_hl_{tag}")
                s_dn = sem(f"s_dn_{tag}")
                s_dnv = sem(f"s_dnv_{tag}")
                s_xe = [sem(f"s_xe{b}_{tag}") for b in range(2)]
                s_tx = sem(f"s_tx_{tag}")
                s_txh = sem(f"s_txh_{tag}")
                s_txl = sem(f"s_txl_{tag}")
                s_eu = sem(f"s_eu_{tag}")
                s_es = sem(f"s_es_{tag}")
                s_em = sem(f"s_em_{tag}")
                s_th = sem(f"s_th_{tag}")
                s_thh = sem(f"s_thh_{tag}")
                s_thl = sem(f"s_thl_{tag}")
                s_ed = sem(f"s_ed_{tag}")
                s_ye = sem(f"s_ye_{tag}")
                s_yst = [sem(f"s_yst{b}_{tag}") for b in range(2)]
                s_add = sem(f"s_add_{tag}")
                s_out = None if first else sem("s_out")

                jobs = []
                if first:
                    for c in range(SC - 1):
                        cols = slice(c * CH, (c + 1) * CH if c < SC - 2 else WGU)
                        jobs.append((wgu[:, cols], wgu_h[:, cols], wgu_l[:, cols]))
                    for a in range(0, SC, 3):
                        jobs.append((wd[:, a:a + 3, :], wd_h[:, a:a + 3, :], wd_l[:, a:a + 3, :]))
                    early = len(jobs)
                    for e in range(NE):
                        jobs.append((w1[:, e], w1_h[:, e], w1_l[:, e]))
                else:
                    early = 0
                for e in range(NE):
                    jobs.append((w2[:, e], w2_h[:, e], w2_l[:, e]))
                by_pool = set(POOL_JOBS_FIRST + POOL_LATE if first else POOL_JOBS_SECOND)

                def lows(q, pool_side):
                    return sum((r in by_pool) == pool_side for r in range(q + 1))

                def wait_low(eng, q):
                    if lows(q, False):
                        eng.wait_ge(s_wl, lows(q, False))
                    if lows(q, True):
                        eng.wait_ge(s_wlp, lows(q, True))


                def flat(ap):
                    return ap.rearrange("p a b -> p (a b)") if len(ap.shape) == 3 else ap

                def job_high(act, q):
                    src, high, _ = jobs[q]
                    act.wait_ge(s_stage[q % NST], 16 * (q // NST + 1))
                    rows, cols = flat(high).shape
                    act.activation(flat(high), stage[q % NST][0:rows, 0:cols], ACT.Copy).then_inc(s_wh, 1)

                def job_low(eng, q, done):
                    _, high, low = jobs[q]
                    eng.wait_ge(s_wh, q + 1)
                    rows, cols = flat(high).shape
                    eng.tensor_tensor(flat(low), stage[q % NST][0:rows, 0:cols], flat(high).bitcast(FP32),
                                      ALU.subtract).then_inc(done, 1)

                def y_buf(j):
                    b = Y_BUF[j]
                    return xn[:, 2 * b:2 * b + 2, :] if b < 4 else rows[:, 2 * (b - 4):2 * (b - 4) + 2, :]

                def y_count(j):
                    return 16 * (y_in[Y_BUF[j]] + 1 + Y_BUF[:j].count(Y_BUF[j]))

                def pair_added(j):
                    return 2 * TOP_K * (j // 2 + 1)

                cuts = CUTS_FIRST if first else CUTS_SECOND
                before = range(0, cuts[0])
                late_of = [range(a, b) for a, b in zip(cuts, cuts[1:] + (len(jobs),))]

                def attention_high(act, t):
                    if t == 0:
                        act.wait_ge(s_wraw, 16)
                    cols = slice(t * (QKV // 3), (t + 1) * (QKV // 3))
                    act.activation(area_h[:, cols], w_raw[:, cols], ACT.Copy).then_inc(s_qh, 2)

                def attention_low(pool, t):
                    pool.wait_ge(s_qh, 2 * (t + 1))
                    cols = slice(t * (QKV // 3), (t + 1) * (QKV // 3))
                    ins = pool.tensor_tensor(area_l[:, cols], w_raw[:, cols], area_h[:, cols].bitcast(FP32),
                                             ALU.subtract)
                    if t >= 1:
                        ins.then_inc(s_ql, 1)

                block_ctx = ExitStack()
                block = block_ctx.enter_context(nc.Block())

                @block.sync
                def _(sp):
                    if first:
                        xv = x_in.rearrange("(j p) d -> p j d", p=P)

                        def load_x(j):
                            sp.dma_start(x_res[:, j:j + 2, :], xv[:, j:j + 2, :]).then_inc(s_x[j // 2], 16)

                        load_x(0)
                        sp.dma_start(cst[:, 0:C_U], consts[:, 0:C_U]).then_inc(s_cst, 16)
                        load_x(2)
                        sp.dma_start(wg_raw, wgate).then_inc(s_gate_in, 16)
                    for q, (src, high, _) in enumerate(jobs):
                        if q >= NST:
                            wait_low(sp, q - NST)
                        rows, cols = flat(high).shape
                        sp.dma_start(stage[q % NST][0:rows, 0:cols], flat(src)).then_inc(s_stage[q % NST], 16)
                        if first and q == 0:
                            for j in range(HT, NT, 2):
                                load_x(j)
                            sp.dma_start(cst[:, C_U:C_N], consts[:, C_U:C_N]).then_inc(s_cst2, 16)
                        if q in XN_OUT:
                            j = XN_OUT.index(q) * HT
                            sp.wait_ge(n["xn"], j + HT)
                            sp.dma_start(xd.rearrange("(j p) d -> p j d", p=P)[:, j:j + HT, :],
                                         xn[:, j:j + HT, :]).then_inc(s_xd, 16)

                    if after:
                        wait_low(sp, len(jobs) - 1)
                        sp.dma_start(w_raw, wqkv[0]).then_inc(s_wraw, 16)
                        sp.dma_start(bias_all[:, :, :], bqkv).then_inc(s_b, 16)
                        sp.dma_start(wo_raw, wo[0]).then_inc(s_woraw, 16)
                    sp.wait_ge(s_yst[0], 16 * ((NM + 1) // 2))
                    sp.wait_ge(s_yst[1], 16 * (NM // 2))
                    for j in range(NT):
                        if Y_BUF[j] in Y_BUF[:j]:
                            sp.wait_ge(s_add, pair_added(Y_BUF.index(Y_BUF[j])))
                        sp.dma_start(y_buf(j), yd[VOID * P:, :].rearrange("(t j p) d -> j p t d", t=TOP_K, p=P)[j]
                                     ).then_inc(s_y[Y_BUF[j]], 16)
                    if not first:
                        ov = out.rearrange("(j p) d -> p j d", p=P)
                        for j in range(NT):
                            sp.wait_ge(s_add, pair_added(j))
                            sp.wait_ge(s_dnv, j + 1)
                            sp.dma_start(ov[:, j, :], x_res[:, j, :]).then_inc(s_out, 16)
                        sp.wait_ge(s_out, 16 * NT)

                @block.gpsimd
                def _(pool):
                    if first:
                        pool.wait_ge(s_cst, 16)
                        norm_rstd(pool, n, 0)
                    norm_rstd(pool, n, 1)
                    late_lows = POOL_LATE if first else ()
                    for q in sorted(by_pool - set(late_lows)):
                        job_low(pool, q, s_wlp)
                    pool.wait_ge(s_xd, 32)
                    pool.wait_ge(s_tok, 1)

                    def gather(m):
                        if m >= 2:
                            pool.wait_ge(s_tx, m - 1)
                        pool.indirect_dma_start(
                            xe[m % 2], None, xd,
                            bass.IndirectOffsetOnAxis(ap=tok_i[:, m:m + 1], axis=0)).then_inc(s_xe[m % 2], 16)

                    def scatter(m):
                        pool.wait_ge(s_ye, m + 1)
                        pool.indirect_dma_start(
                            yd, bass.IndirectOffsetOnAxis(ap=place[:, m:m + 1], axis=0),
                            ye[m % 2], None).then_inc(s_yst[m % 2], 16)

                    for m in range(NM + OUT_LAG):
                        if m == 2:
                            for q in late_lows:
                                job_low(pool, q, s_wlp)
                        if m < NM:
                            gather(m)
                        if m >= OUT_LAG:
                            scatter(m - OUT_LAG)
                    if after:
                        for t in range(3):
                            attention_low(pool, t)
                        norm_rstd(pool, after, 0)

                @block.scalar
                def _(act):
                    if first:
                        act.wait_ge(s_gate_in, 16)
                        act.activation(flat(wg_h[:, :, :]), wg_raw, ACT.Copy).then_inc(s_gh, 1)
                        job_high(act, 0)
                        norm_high(act, n, 0, (0, 1))
                        for q in before[1:]:
                            job_high(act, q)

                    def logits_out(half):
                        act.wait_ge(s_lgt, half + 1)
                        for a in range(2):
                            act.activation(lgT[2 * half + a][0:NG, :], bank[6][0:NG, a * D:(a + 1) * D],
                                           ACT.Copy).then_inc(s_lgt_sb, 1)

                    def shared_silu(c):
                        act.wait_ge(s_up, c + 1)
                        if c >= 2:
                            act.wait_ge(s_hl, c - 1)
                        if c % SC < SC - 1:
                            act.activation(hs[c % 2][:, :], bank[2 * (c % 2)][:, :], ACT.Silu).then_inc(s_silu, 1)
                        else:
                            act.activation(hs[c % 2][0:LASTW, :], bank[2 * (c % 2)][LASTW:P, :],
                                           ACT.Silu).then_inc(s_silu, 1)

                    def width(c):
                        return P if c % SC < SC - 1 else LASTW

                    def shared_high(c):
                        act.wait_ge(s_hm, c + 1)
                        w = width(c)
                        if c == SC:
                            act.wait_ge(s_dn, NT // 2)
                        act.activation(hT_h[0:w, c % SC, :], hs[c % 2][0:w, :], ACT.Copy).then_inc(s_hh, 1)

                    def tile_high(m, b):
                        act.wait_ge(s_tx, m + 1)
                        act.activation(xeT_h[b][:, :], bank[b][:, 0:KD * P], ACT.Copy).then_inc(s_txh, 1)

                    def gate_exps():
                        act.wait_ge(s_route, R1)
                        act.activation(gates[:, 0, :], best2[:, :], ACT.Exp).then_inc(s_exp, 1)
                        act.activation(gates[:, 1, :], lg[:, :, NE], ACT.Exp, scale=-1.0).then_inc(s_exp, 1)

                    logits_out(0)
                    shared_silu(0)
                    for q in late_of[0]:
                        job_high(act, q)
                    norm_high(act, n, 1, (4, 5))
                    shared_high(0)
                    shared_silu(1)
                    logits_out(1)
                    for q in late_of[1]:
                        job_high(act, q)
                    shared_high(1)
                    for c in range(2, SC):
                        shared_silu(c)
                        if c < SC - 1:
                            for q in late_of[c]:
                                job_high(act, q)
                        shared_high(c)
                    gate_exps()
                    for q in late_of[SC - 1]:
                        job_high(act, q)
                    for c in range(SC, SC + AHEAD):
                        shared_silu(c)
                        for q in late_of[c]:
                            job_high(act, q)
                        if c == SC + AHEAD - 1:
                            tile_high(0, 0)
                        shared_high(c)

                    def inner_high(m, b):
                        act.wait_ge(s_th, m + 1)
                        act.activation(heT_h[b][:, :], bank[4 + b][0:IC, 0:2 * P], ACT.Copy).then_inc(s_thh, 1)

                    def inner_silu(m, b):
                        act.wait_ge(s_eu, m + 1)
                        act.activation(he[b][:, :], bank[2 + b][:, 0:IM], ACT.Silu).then_inc(s_es, 1)

                    def tile_out(m, q, b, guard=True):
                        act.wait_ge(s_ed, m + 1)
                        if guard:
                            act.wait_ge(s_yst[b], 16 * q)
                        act.activation(ye[b][:, :], bank[6 + b][:, 0:D], ACT.Copy).then_inc(s_ye, 1)

                    def step(m, q, b, guard=True):
                        tile_high(m + 1, 1 - b)
                        inner_silu(m, b)
                        inner_high(m - 1, 1 - b)
                        tile_out(m - 2, q - 1, b, guard)

                    tile_high(1, 1)
                    inner_silu(0, 0)
                    tile_high(2, 0)
                    inner_silu(1, 1)
                    inner_high(0, 0)
                    step(2, 1, 0, False)
                    step(3, 1, 1, False)
                    with act.Fori(2, NM // 2) as i:
                        step(2 * i, i, 0)
                        step(2 * i + 1, i, 1)
                    m = NM - 1
                    inner_silu(m, 0)
                    inner_high(m - 1, 1)
                    tile_out(m - 2, m // 2 - 1, 0)
                    inner_high(m, 0)
                    tile_out(m - 1, m // 2 - 1, 1)
                    tile_out(m, m // 2, 0)
                    if after:
                        for t in range(3):
                            attention_high(act, t)
                    for c in range(SC + AHEAD, 2 * SC):
                        shared_silu(c)
                        shared_high(c)
                    if after:
                        norm_high(act, after, 0, (4, 5))

                @block.vector
                def _(dve):
                    steps = [0]

                    def link(ins):
                        steps[0] += 1
                        ins.then_inc(s_route, 1)
                        dve.wait_ge(s_route, steps[0])

                    def wide(ap):
                        return ap.unsqueeze(2).to_broadcast([P, NT, NE])

                    desc = cst[:, C_DESC:C_DESC + NE].unsqueeze(1).to_broadcast([P, NT, NE])

                    def route():
                        dve.wait_ge(s_logits, 1)
                        link(dve.tensor_copy(flat(lg[:, :, :]), bank[4][:, 0:NT * NG]))
                        link(dve.tensor_reduce(best[:, :], lg[:, :, 0:NE], op=ALU.max, axis=AX.X))
                        link(dve.tensor_tensor(dl[:, :, :], lg[:, :, 0:NE], wide(best[:, :]), ALU.subtract))
                        link(dve.scalar_tensor_tensor(sc[:, :, :], dl[:, :, :], 0.0, desc, ALU.is_ge, ALU.mult))
                        link(dve.tensor_reduce(lead[:, :], sc[:, :, :], op=ALU.max, axis=AX.X))
                        link(dve.tensor_tensor(sel[:, 0], sc[:, :, :], wide(lead[:, :]), ALU.is_equal))
                        link(dve.scalar_tensor_tensor(dl[:, :, :], sel[:, 0], -BIG, dl[:, :, :], ALU.mult, ALU.add))
                        link(dve.tensor_reduce(best2[:, :], dl[:, :, :], op=ALU.max, axis=AX.X))
                        assert steps[0] == R1
                        link(dve.tensor_tensor(dl[:, :, :], dl[:, :, :], wide(best2[:, :]), ALU.is_equal))
                        link(dve.tensor_tensor(sc[:, :, :], dl[:, :, :], desc, ALU.mult))
                        link(dve.tensor_reduce(lead[:, :], sc[:, :, :], op=ALU.max, axis=AX.X))
                        link(dve.tensor_tensor(sel[:, 1], sc[:, :, :], wide(lead[:, :]), ALU.is_equal))
                        dve.tensor_tensor(assigned[:, 0:NT, :], sel[:, 0], sel[:, 1], ALU.add).then_inc(s_assigned, 1)

                    def shared_mul(c):
                        dve.wait_ge(s_silu, c + 1)
                        if c % SC < SC - 1:
                            dve.tensor_tensor(hs[c % 2][:, :], hs[c % 2][:, :], bank[2 * (c % 2) + 1][:, :],
                                              ALU.mult).then_inc(s_hm, 1)
                        else:
                            dve.tensor_tensor(hs[c % 2][0:LASTW, :], hs[c % 2][0:LASTW, :],
                                              bank[2 * (c % 2)][0:LASTW, :], ALU.mult).then_inc(s_hm, 1)

                    def shared_low(c):
                        dve.wait_ge(s_hh, c + 1)
                        w = P if c % SC < SC - 1 else LASTW
                        dve.tensor_tensor(hT_l[0:w, c % SC, :], hs[c % 2][0:w, :],
                                          hT_h[0:w, c % SC, :].bitcast(FP32), ALU.subtract).then_inc(s_hl, 1)

                    def shared_out(j):
                        dve.wait_ge(s_dn, j + 1)
                        dve.scalar_tensor_tensor(x_res[:, j, :], bank[6 + j % 2][:, 0:D], gates_r[:, 1, j:j + 1],
                                                 x_res[:, j, :], ALU.mult, ALU.add).then_inc(s_dnv, 1)

                    def slots():
                        dve.wait_ge(s_rank, 1)
                        rank = bank[5][:, 0:(NT + 1) * NE].rearrange("p (a b) -> p a b", b=NE)
                        link(dve.tensor_tensor(cmp[:, :, :], wide(rank[:, NT, :]),
                                               cst[:, C_M128:C_M128 + NT].unsqueeze(1).to_broadcast([P, NE, NT]),
                                               ALU.is_gt))
                        link(dve.tensor_reduce(tiles_of[:, :], cmp[:, :, :], op=ALU.add, axis=AX.X))
                        link(dve.tensor_tensor(cmp[:, :, :], tiles_of[:, :].unsqueeze(1).to_broadcast([P, NE, NE]),
                                               cst[:, C_LT:C_LT + NE * NE].rearrange("p (a b) -> p a b", a=NE),
                                               ALU.mult))
                        link(dve.tensor_reduce(base[:, :], cmp[:, :, :], op=ALU.add, axis=AX.X))
                        link(dve.scalar_tensor_tensor(slot[:, :, :],
                                                      base[:, :].unsqueeze(1).to_broadcast([P, NT, NE]), float(P),
                                                      rank[:, 0:NT, :], ALU.mult, ALU.add))
                        link(dve.tensor_tensor(sel[:, :, :, :].rearrange("p t a b -> p t (a b)"),
                                               sel[:, :, :, :].rearrange("p t a b -> p t (a b)"),
                                               flat(slot[:, :, :]).unsqueeze(1).to_broadcast([P, TOP_K, NT * NE]),
                                               ALU.mult))
                        dve.tensor_reduce(slot_f[:, :], sel[:, :, :, :].rearrange("p t a b -> p (t a) b"),
                                          op=ALU.add, axis=AX.X).then_inc(s_route, 1)
                        steps[0] += 1
                        dve.wait_ge(s_route, steps[0])
                        dve.tensor_copy(slot_i[:, :], slot_f[:, :]).then_inc(s_slot, 1)
                        dve.wait_ge(s_slot, 1)
                        copies = [P, TOP_K * NT, NM]
                        dve.tensor_scalar(slot_tile[:, :], slot_i[:, :], -P, None, ALU.bitwise_and).then_inc(s_slot, 1)
                        dve.tensor_scalar(slot_row[:, :], slot_i[:, :], P - 1, None, ALU.bitwise_and).then_inc(s_slot, 1)
                        dve.wait_ge(s_slot, 2)
                        link(dve.tensor_tensor(tile_hot[:, :, :], slot_tile[:, :].unsqueeze(2).to_broadcast(copies),
                                               cst[:, C_MP:C_MP + NM].unsqueeze(1).to_broadcast(copies),
                                               ALU.is_equal))
                        dve.tensor_scalar(token_hot[:, :, 0, :], tile_hot[:, :, :], cst[:, C_P:C_P + 1], None,
                                          ALU.mult).then_inc(s_hot, 1)
                        dve.tensor_tensor(token_hot[:, :, 1, :], tile_hot[:, :, :],
                                          cst[:, C_J:C_J + TOP_K * NT].unsqueeze(2).to_broadcast(copies),
                                          ALU.mult).then_inc(s_hot, 1)

                    def rows_of_slots():
                        dve.wait_ge(s_slot, 3)
                        copies = [P, TOP_K * NT, P]
                        dve.tensor_tensor(row_hot, slot_row[:, :].unsqueeze(2).to_broadcast(copies),
                                          cst[:, C_COL:C_COL + P].unsqueeze(1).to_broadcast(copies),
                                          ALU.is_equal).then_inc(s_hot, 1)

                    def tile_experts():
                        dve.wait_ge(s_hot, 2)
                        link(dve.tensor_tensor(end[:, :], base[:, :], tiles_of[:, :], ALU.add))
                        link(dve.tensor_tensor(tile_cmp[0:1, :, :],
                                               cst[0:1, C_MI:C_MI + NM].unsqueeze(2).to_broadcast([1, NM, NE]),
                                               end[0:1, :].unsqueeze(1).to_broadcast([1, NM, NE]), ALU.is_ge))
                        link(dve.tensor_reduce(tile_f[0:1, :], tile_cmp[0:1, :, :], op=ALU.add, axis=AX.X))
                        dve.tensor_scalar(tile_e[0:1, :], tile_f[0:1, :], float(NE - 1), None,
                                          ALU.min).then_inc(s_expert, 1)

                    def tokens():
                        dve.wait_ge(s_inv, 1)
                        code = bank[5][:, NM:2 * NM]
                        link(dve.scalar_tensor_tensor(tok_f, code, 0.0, cst[:, C_VOID:C_VOID + NM],
                                                      ALU.is_equal, ALU.mult))
                        link(dve.tensor_tensor(tok_f, bank[5][:, 0:NM], tok_f, ALU.add))
                        link(dve.scalar_tensor_tensor(place[:, :], code, float(P), tok_f, ALU.mult, ALU.add))
                        dve.tensor_scalar(tok_i[:, :], place[:, :], TOK - 1, None,
                                          ALU.bitwise_and).then_inc(s_tok, 1)

                    def weights():
                        dve.wait_ge(s_exp, 2)
                        link(dve.tensor_scalar(gates_r[:, :, :], gates[:, :, :], 1.0, None, ALU.add))
                        link(dve.reciprocal(gates_r[:, :, :], gates_r[:, :, :]))
                        link(dve.tensor_scalar(gates_r[:, :, :], gates_r[:, :, :], 0.5, None, ALU.mult))
                        link(dve.tensor_tensor(cw2[:, :], gates[:, 0, :], gates_r[:, 0, :], ALU.mult))

                    def tile_low(m, b):
                        dve.wait_ge(s_txh, m + 1)
                        dve.tensor_tensor(xeT_l[b][:, :], bank[b][:, 0:KD * P], xeT_h[b][:, :].bitcast(FP32),
                                          ALU.subtract).then_inc(s_txl, 1)

                    def lows_of(qs):
                        for q in qs:
                            if q not in by_pool:
                                job_low(dve, q, s_wl)

                    if first:
                        dve.memset(token_hot[:, :, :, :].rearrange("p a b c -> p (a b c)"), 0.0).then_inc(s_zero, 1)
                        norm_stats(dve, n, 0, s_x)
                        norm_apply(dve, n, 0)
                        norm_stats(dve, n, 1, s_x)
                        dve.wait_ge(s_gh, 1)
                        dve.tensor_tensor(flat(wg_l[:, :, :]), wg_raw, flat(wg_h[:, :, :]).bitcast(FP32),
                                          ALU.subtract).then_inc(s_gl, 1)
                        lows_of(before[0:1])
                        norm_low(dve, n, 0, (0, 1))
                        lows_of(before[1:])
                        dve.wait_ge(s_cst2, 16)
                        dve.tensor_copy(rank_w[:, :, :].rearrange("p a b -> p (a b)"),
                                        cst[:, C_U:C_ONE + P]).then_inc(s_rw, 1)
                    else:
                        norm_stats(dve, n, 1)
                    dve.memset(assigned[:, NT, :], 0.0).then_inc(s_rw, 1)
                    norm_apply(dve, n, 1)
                    lows_of(late_of[0])
                    shared_mul(0)
                    norm_low(dve, n, 1, (4, 5))
                    shared_low(0)
                    shared_mul(1)
                    route()
                    lows_of(late_of[1])
                    shared_low(1)
                    for c in range(2, SC):
                        shared_mul(c)
                        if c == 2:
                            slots()
                        if c == 3:
                            rows_of_slots()
                        if c == INV_AT:
                            tokens()
                        if c < SC - 1:
                            lows_of(late_of[c])
                        shared_low(c)
                    tile_experts()
                    weights()
                    for j in range(NT // 2):
                        some = -(-len(late_of[SC - 1]) // (NT // 2))
                        lows_of(late_of[SC - 1][some * j:some * (j + 1)])
                        shared_out(j)
                    for c in range(SC, SC + AHEAD):
                        shared_mul(c)
                        lows_of(late_of[c])
                        if c == SC + AHEAD - 1:
                            tile_low(0, 0)
                        shared_low(c)

                    def inner_low(m, b):
                        dve.wait_ge(s_thh, m + 1)
                        dve.tensor_tensor(heT_l[b][:, :], bank[4 + b][0:IC, 0:2 * P], heT_h[b][:, :].bitcast(FP32),
                                          ALU.subtract).then_inc(s_thl, 1)

                    def inner_mul(m, b):
                        dve.wait_ge(s_es, m + 1)
                        dve.tensor_tensor(he[b][:, :], he[b][:, :], bank[2 + b][:, IM:2 * IM],
                                          ALU.mult).then_inc(s_em, 1)

                    tile_low(1, 1)
                    inner_mul(0, 0)
                    with dve.Fori(0, (NM - 3) // 2) as i:
                        for b in range(2):
                            m = 2 * i + 1 + b
                            tile_low(m + 1, b)
                            inner_mul(m, 1 - b)
                            inner_low(m - 1, b)
                    m = NM - 2
                    tile_low(m + 1, 0)
                    inner_mul(m, 1)
                    inner_low(m - 1, 0)
                    inner_mul(m + 1, 0)
                    inner_low(m, 1)
                    inner_low(m + 1, 0)

                    def add(h):
                        a, t = divmod(h, TOP_K)
                        for j in (2 * a, 2 * a + 1):
                            if t == 0:
                                dve.wait_ge(s_y[Y_BUF[j]], y_count(j))
                            else:
                                dve.wait_ge(s_add, pair_added(j) - 4 + j % 2 + 1)
                            w = gates_r[:, 0, j:j + 1] if t == 0 else cw2[:, j:j + 1]
                            dve.scalar_tensor_tensor(x_res[:, j, :], y_buf(j)[:, t, :], w, x_res[:, j, :],
                                                     ALU.mult, ALU.add).then_inc(s_add, 1)

                    dve.wait_ge(s_dnv, NT // 2)
                    added = 0
                    for c in range(SC + AHEAD, 2 * SC):
                        shared_mul(c)
                        for _ in range(ADDS[c - SC]):
                            add(added)
                            added += 1
                        shared_low(c)
                    for j in (NT // 2, NT // 2 + 1):
                        shared_out(j)
                    for h in range(added, NT // 2):
                        add(h)
                    if after:
                        dve.wait_ge(s_add, NT)
                        norm_stats(dve, after, 0)
                    dve.wait_ge(s_dnv, NT // 2 + 2)
                    for h in range(NT // 2, NT // 2 + TOP_K):
                        add(h)
                    if after:
                        norm_apply(dve, after, 0)
                    for h in range(NT // 2 + TOP_K, NT):
                        add(h)
                    dve.wait_ge(s_add, TOP_K * NT)
                    for j in (NT - 2, NT - 1):
                        shared_out(j)
                    if after:
                        norm_low(dve, after, 0, (4, 5))

                @block.tensor
                def _(pe):
                    if first:
                        pe.wait_ge(s_zero, 1)
                        some = token_hot[:, :, :, :].rearrange("p a b c -> p (a b c)")
                        for _ in range(WARM[0]):
                            pe.matmul(bank[7][:, :], some[:, 0:P], some[:, 0:HALF], start=True, stop=True)
                        pe.wait_ge(s_cst, 16)
                        norm_turn(pe, n, 0, (0, 1))
                        for _ in range(WARM[1]):
                            pe.matmul(bank[7][:, :], some[:, 0:P], some[:, 0:HALF], start=True, stop=True)
                        norm_wait(pe, n, 0)
                        pe.wait_ge(s_gh, 1)
                        pe.wait_ge(s_gl, 1)

                    def logits(half):
                        if half:
                            pe.wait_ge(s_lgt_sb, 2)
                        toks = slice(half * HALF, (half + 1) * HALF)
                        for k in range(KD):
                            last = split_matmuls(pe, bank[6][:, :], (wg_h[:, k, :], wg_l[:, k, :]),
                                                 (xT_h[:, k, toks], xT_l[:, k, toks]), k == 0, k == KD - 1)
                        last.then_inc(s_lgt, 1)

                    def shared_up(c):
                        half, ch = divmod(c, SC)
                        if c >= 2:
                            pe.wait_ge(s_hm, c - 1)
                        if first and c < SC - 1:
                            pe.wait_ge(s_wh, c + 1)
                            wait_low(pe, c)
                        toks = slice(half * HALF, (half + 1) * HALF)
                        for g in range(2 if ch < SC - 1 else 1):
                            for k in range(KD):
                                at = ch * CH + (g * KD + k) * P
                                last = split_matmuls(pe, bank[2 * (c % 2) + g][:, :],
                                                     (wgu_h[:, at:at + P], wgu_l[:, at:at + P]),
                                                     (xT_h[:, k, toks], xT_l[:, k, toks]), k == 0, k == KD - 1)
                        last.then_inc(s_up, 1)

                    def shared_down(half):
                        for j0 in (4 * half, 4 * half + 2):
                            for cs in (range(SC - 1), range(SC - 1, SC)):
                                for j in (j0, j0 + 1):
                                    if j % 4 >= 2 and cs[0] == 0:
                                        pe.wait_ge(s_dnv, j - 1)
                                    toks = slice((j % 4) * P, (j % 4 + 1) * P)
                                    for c in cs:
                                        if j == 4 * half:
                                            pe.wait_ge(s_hh, SC * half + c + 1)
                                            pe.wait_ge(s_hl, SC * half + c + 1)
                                        w = P if c < SC - 1 else LASTW
                                        last = split_matmuls(pe, bank[6 + j % 2][:, 0:D],
                                                             (hT_h[0:w, c, toks], hT_l[0:w, c, toks]),
                                                             (wd_h[0:w, c, :], wd_l[0:w, c, :]),
                                                             c == 0, c == SC - 1)
                                    if c == SC - 1:
                                        last.then_inc(s_dn, 1)

                    logits(0)
                    shared_up(0)
                    norm_turn(pe, n, 1, (4, 5))
                    shared_up(1)
                    norm_wait(pe, n, 1)
                    logits(1)
                    pe.wait_ge(s_lgt_sb, 4)
                    for j in range(NT):
                        last = pe.transpose(bank[4][:, j * NG:(j + 1) * NG],
                                            lgT[j // 2][0:NG, (j % 2) * P:(j % 2 + 1) * P],
                                            cst[0:NG, C_ID:C_ID + NG])
                    last.then_inc(s_logits, 1)
                    shared_up(2)
                    pe.wait_ge(s_rw, 2 if first else 1)
                    pe.wait_ge(s_assigned, 1)
                    pe.matmul(bank[5][:, 0:(NT + 1) * NE], rank_w[:, 0, :],
                              assigned[:, :, :].rearrange("p a b -> p (a b)"), start=True, stop=False)
                    for j in range(NT):
                        last = pe.matmul(bank[5][:, (j + 1) * NE:(NT + 1) * NE], rank_w[:, 1, :],
                                         assigned[:, j, :].unsqueeze(1).to_broadcast([P, NT - j, NE]),
                                         start=False, stop=j == NT - 1)
                    last.then_inc(s_rank, 1)
                    for c in range(3, SC):
                        shared_up(c)
                        if c == INV_AT:
                            pe.wait_ge(s_hot, 3)
                            for q in range(TOP_K * NT):
                                last = pe.matmul(bank[5][:, 0:2 * NM], row_hot[:, q, :],
                                                 token_hot[:, q, :, :].rearrange("p a b -> p (a b)"),
                                                 start=q == 0, stop=q == TOP_K * NT - 1)
                            last.then_inc(s_inv, 1)
                    if first:
                        wait_low(pe, early - 1)
                    shared_up(SC)
                    shared_down(0)
                    for c in range(SC + 1, SC + AHEAD):
                        shared_up(c)

                    def tile_in(m, q, b):
                        pe.wait_ge(s_xe[b], 16 * (q + 1))
                        for k in range(KD):
                            last = pe.transpose(bank[b][:, k * P:(k + 1) * P], xe[b][:, k * P:(k + 1) * P], ident)
                        last.then_inc(s_tx, 1)

                    e_up, e_turn, e_down = [pe.alloc_register(f"e_{x}_{tag}") for x in ("up", "turn", "down")]

                    def expert(reg):
                        return pe.snap(reg, min_val=0, max_val=NE - 1)

                    def next_experts(m):
                        pe.reg_mov(e_down, e_turn)
                        pe.reg_mov(e_turn, e_up)
                        pe.reg_load(e_up, tile_e[0:1, bass.ds(m, 1)])

                    def up(m, b):
                        e = expert(e_up)
                        pe.wait_ge(s_txh, m + 1)
                        pe.wait_ge(s_txl, m + 1)
                        for k in range(KD):
                            part = slice(k * P, (k + 1) * P)
                            last = split_matmuls(pe, bank[2 + b][:, 0:2 * IM],
                                                 (xeT_h[b][:, part], xeT_l[b][:, part]),
                                                 (w1_h[:, e, k, :], w1_l[:, e, k, :]), k == 0, k == KD - 1)
                        last.then_inc(s_eu, 1)

                    def inner_turn(m, b):
                        pe.wait_ge(s_em, m + 1)
                        for c in range(2):
                            last = pe.transpose(bank[4 + b][0:IC, c * P:(c + 1) * P],
                                                he[b][:, c * IC:(c + 1) * IC], ident)
                        last.then_inc(s_th, 1)

                    def down(m, b, guard=True, more=True):
                        e = expert(e_down)
                        pe.wait_ge(s_thh, m + 1)
                        pe.wait_ge(s_thl, m + 1)
                        if guard:
                            pe.wait_ge(s_ye, m - 1)
                        for c in range(2):
                            part = slice(c * P, (c + 1) * P)
                            last = split_matmuls(pe, bank[6 + b][:, 0:D],
                                                 (heT_h[b][:, part], heT_l[b][:, part]),
                                                 (w2_h[:, e, c, :], w2_l[:, e, c, :]), c == 0, c == 1)
                            if c == 0 and more:
                                next_experts(m + 3)
                        last.then_inc(s_ed, 1)

                    def step(m, q, b, guard=True):
                        tile_in(m + 1, q + b, 1 - b)
                        up(m, b)
                        inner_turn(m - 1, 1 - b)
                        down(m - 2, b, guard)

                    assert AHEAD == 2
                    pe.wait_ge(s_hm, SC + AHEAD - 1)
                    tile_in(0, 0, 0)
                    tile_in(1, 0, 1)
                    pe.wait_ge(s_hm, SC + AHEAD)
                    if first:
                        keep_warm(pe, 5, WARM[2])
                        pe.wait_ge(s_wh, early + NE)
                        wait_low(pe, early + NE - 1)
                    pe.wait_ge(s_expert, 1)
                    pe.wait_ge(s_dnv, NT // 2)
                    for reg in (e_up, e_turn):
                        pe.reg_load(reg, tile_e[0:1, 0:1])
                    up(0, 0)
                    next_experts(1)
                    tile_in(2, 1, 0)
                    up(1, 1)
                    next_experts(2)
                    inner_turn(0, 0)
                    pe.wait_ge(s_wh, len(jobs))
                    wait_low(pe, len(jobs) - 1)
                    step(2, 1, 0, False)
                    step(3, 1, 1, False)
                    assert (NM - 5) % STEPS == 0
                    with pe.Fori(0, (NM - 5) // STEPS) as i:
                        for k in range(STEPS):
                            step(STEPS * i + 4 + k, STEPS // 2 * i + 2 + k // 2, k % 2)
                    m = NM - 1
                    up(m, 0)
                    inner_turn(m - 1, 1)
                    down(m - 2, 0, more=False)
                    next_experts(m)
                    inner_turn(m, 0)
                    down(m - 1, 1, more=False)
                    next_experts(m)
                    down(m, 0, more=False)
                    for c in range(SC + AHEAD, 2 * SC):
                        shared_up(c)
                    pe.wait_ge(s_ye, NM)
                    shared_down(1)
                    if after:
                        keep_warm(pe, 1, WARM[3])
                        norm_turn(pe, after, 0, (4, 5))

                block_ctx.close()
                for b in Y_BUF:
                    y_in[b] += 1

        def attention():
            loc = ExitStack()
            with loc:
                def sb(name, shape, dt=FP32):
                    return sbuf(f"{name}_a", shape, dt, loc)

                w_h, zT_h, wo_h = [attn_w(area_h, kind) for kind in "wzo"]
                w_l, zT_l, wo_l = [attn_w(area_l, kind) for kind in "wzo"]
                qk = sb("qk", [P, 2, 2, TOK])
                v = sb("v", [P, NT, 2 * DH])
                bias = sb("bias", [P, 3, 2])
                bo_sb = sb("bo_sb", [P, D])
                NS = 5
                s = [sb(f"s{b}", [P, 3 * P]) for b in range(NS)]
                mn = sb("mn", [P, NS, 2])
                rs = sb("rs", [P, NS, 2])
                rr = sb("rr", [P, NS, 2])
                pT = [sb(f"pT{b}", [P, 3 * P]) for b in range(2)]

                n = norm2
                s_bo = sem("a_bo")
                s_bp = sem("a_bias_pair")
                s_woh = sem("a_woh")
                s_wol = sem("a_wol")
                s_proj = sem("a_proj")
                s_pa = sem("a_proj_act")
                s_pv = sem("a_proj_dve")
                s_sc = sem("a_scores")
                s_sm = sem("a_masked")
                s_mn = sem("a_min")
                s_e = sem("a_exp")
                s_rr = sem("a_recip")
                s_p = sem("a_probs")
                s_pt = sem("a_pT_psum")
                s_ptv = sem("a_pT")
                s_z = sem("a_z_psum")
                s_zh = sem("a_zh")
                s_zl = sem("a_zl")
                s_o = sem("a_o_psum")
                s_ov = sem("a_o_added")
                U = 2 * BATCH
                PROJ = 12
                ORDER = ("A0 A1 O3 A2 A3 V0 S0 V1 S1 B0 S2 B1 S3 T0 B2 M0 T1 B3 M1 T2 V2 S4 M2 S5 "
                         "T3 V3 M3 S6 O0 T4 S7 M4 T5 O1 M5 T6 M6 T7 O2 M7").split()
                ACT_ORDER = ("A0 A2 V0 E0 E1 B0 E2 T0 E3 B2 Z0 T1 Z1 T2 V2 Z2 E4 T3 E5 Z3 T4 E6 Z4 T5 E7 Z5 "
                             "T6 Z6 T7 Z7").split()
                DVE_ORDER = ("A1 O3 A3 K0 V1 K1 R0 K2 B1 R1 K3 R2 L0 R3 B3 L1 K4 L2 K5 R4 V3 L3 K6 R5 K7 O0 L4 R6 "
                             "O1 L5 R7 L6 O2 L7").split()
                BANKED = [item for item in ORDER if item[0] in "ABVO"]
                BANK = {item: at % 2 for at, item in enumerate(BANKED)}
                ON_ACT = [item for item in ACT_ORDER if item[0] in "ABV"]
                ON_DVE = [item for item in DVE_ORDER if item[0] in "ABV"]
                PROJECTED = [item for item in ORDER if item[0] in "ABV"]

                ZB = (2, 7)

                def unit(u):
                    return u // 2, u % 2

                block_ctx = ExitStack()
                block = block_ctx.enter_context(nc.Block())

                @block.sync
                def _(sp):
                    sp.dma_start(bo_sb[:, :], bo.partition_broadcast(P)).then_inc(s_bo, 16)
                    with sp.Fori(1, NP) as i:
                        sp.wait_ge(s_ql, 2 * i)
                        sp.dma_start(w_raw, wqkv[i]).then_inc(s_wraw, 16)
                        sp.wait_ge(s_wol, i)
                        sp.dma_start(wo_raw, wo[i]).then_inc(s_woraw, 16)

                PIECE = QKV // 6
                SPLIT_AFTER = (1, 2, 3, 7)
                zero = cst[:, C_ZERO:C_ZERO + 1]

                @block.gpsimd
                def _(pool):
                    def w_flat(t):
                        return t[:, :, :, :].rearrange("p a b c -> p (a b c)")

                    def o_flat(t):
                        return t[:, :, :].rearrange("p a b -> p (a b)")

                    def split_qkv(i, c):
                        if c == 0:
                            pool.wait_ge(s_wraw, 16 * (i + 1))
                        last_use = PROJECTED.index(("B1", "B3", "V3")[c // 2]) + 1
                        pool.wait_ge(s_proj, PROJ * (i - 1) + last_use)
                        cols = slice(c * PIECE, (c + 1) * PIECE)
                        pool.tensor_tensor(w_flat(w_h)[:, cols], w_raw[:, cols], zero.to_broadcast([P, PIECE]),
                                           ALU.add).then_inc(s_qh, 1)
                        pool.wait_ge(s_qh, 6 * i + c + 1)
                        ins = pool.tensor_tensor(w_flat(w_l)[:, cols], w_raw[:, cols],
                                                 w_flat(w_h)[:, cols].bitcast(FP32), ALU.subtract)
                        if c in (3, 5):
                            ins.then_inc(s_ql, 1)

                    norm_rstd(pool, n, 1)

                    def body(i, more):
                        if more != "first":
                            for c in (4, 5):
                                split_qkv(i, c)
                        pool.wait_ge(s_woraw, 16 * (i + 1))
                        if more != "first":
                            pool.wait_ge(s_o, BATCH * i)
                        pool.tensor_tensor(o_flat(wo_h), wo_raw, zero.to_broadcast([P, 2 * D]),
                                           ALU.add).then_inc(s_woh, 1)
                        pool.wait_ge(s_woh, i + 1)
                        pool.tensor_tensor(o_flat(wo_l), wo_raw, o_flat(wo_h).bitcast(FP32),
                                           ALU.subtract).then_inc(s_wol, 1)
                        for u in range(U):
                            pool.wait_ge(s_rr, U * i + u + 1)
                            b = u % NS
                            pool.tensor_tensor(s[b][:, 0:P], s[b][:, 0:P],
                                               rr[:, b, 0:1].to_broadcast([P, P]), ALU.mult).then_inc(s_p, 1)
                            pool.tensor_tensor(s[b][:, P:3 * P], s[b][:, P:3 * P],
                                               rr[:, b, 1:2].to_broadcast([P, 2 * P]), ALU.mult).then_inc(s_p, 1)
                            if more != "last" and u in SPLIT_AFTER:
                                split_qkv(i + 1, SPLIT_AFTER.index(u))

                    body(0, "first")
                    with pool.Fori(1, NP - 1) as i:
                        body(i, "more")
                    body(NP - 1, "last")
                    norm_rstd(pool, norm3, 0)

                def proj_out(item):
                    kind, x = item[0], int(item[1])
                    if kind == "V":
                        return v[:, 2 * x:2 * x + 2, :].rearrange("p a b -> p (a b)")
                    half = "AB".index(kind)
                    return qk[:, x // 2, x % 2, half * HALF:(half + 1) * HALF]

                @block.scalar
                def _(act):
                    def proj(i, item):
                        act.wait_ge(s_proj, PROJ * i + PROJECTED.index(item) + 1)
                        src = bank[BANK[item]][:, :]
                        x = int(item[1])
                        if item[0] == "V":
                            act.activation(proj_out(item), src, ACT.Copy).then_inc(s_pa, 1)
                        else:
                            act.activation(proj_out(item), src, ACT.Identity,
                                           bias=bias[:, x // 2, x % 2:x % 2 + 1]).then_inc(s_pa, 1)

                    def exps(i, u):
                        b = u % NS
                        act.wait_ge(s_mn, 2 * (U * i + u + 1))
                        for t, cols in ((0, slice(0, P)), (1, slice(P, 3 * P))):
                            act.activation(s[b][:, cols], s[b][:, cols], ACT.Exp, bias=mn[:, b, t:t + 1], scale=-1.0,
                                           accum_out=rs[:, b, t:t + 1]).then_inc(s_e, 1)

                    def turned(i, u):
                        act.wait_ge(s_pt, U * i + u + 1)
                        act.activation(pT[u % 2][:, :], bank[5 + u % 2][:, 0:3 * P], ACT.Copy).then_inc(s_ptv, 1)

                    def z_high(i, u):
                        bt, h = unit(u)
                        act.wait_ge(s_z, U * i + u + 1)
                        act.activation(zT_h[:, h, bt * SEQ:(bt + 1) * SEQ], bank[ZB[u % 2]][:, 0:SEQ], ACT.Identity,
                                       bias=bias[:, 2, h:h + 1]).then_inc(s_zh, 1)

                    def body(i, order):
                        act.wait_ge(s_bp, i + 1)
                        for item in order:
                            kind, x = item[0], int(item[1])
                            if kind in "ABV":
                                proj(i, item)
                            else:
                                {"E": exps, "T": turned, "Z": z_high}[kind](i, x)

                    body(0, ACT_ORDER[:1])
                    norm_high(act, n, 1, (5, 6))
                    body(0, ACT_ORDER[1:])
                    with act.Fori(1, NP) as i:
                        body(i, ACT_ORDER)
                    norm_high(act, norm3, 0, (3, 4))

                @block.vector
                def _(dve):
                    norm_stats(dve, n, 1)
                    dve.wait_ge(s_b, 16)
                    dve.tensor_copy(bias[:, :, :], bias_all[:, :, 0:2]).then_inc(s_bp, 1)
                    norm_apply(dve, n, 1)
                    def proj(i, item):
                        dve.wait_ge(s_proj, PROJ * i + PROJECTED.index(item) + 1)
                        src = bank[BANK[item]][:, :]
                        x = int(item[1])
                        if item[0] == "V":
                            dve.tensor_copy(proj_out(item), src).then_inc(s_pv, 1)
                        else:
                            dve.tensor_scalar(proj_out(item), src, bias[:, x // 2, x % 2:x % 2 + 1], None,
                                              ALU.add).then_inc(s_pv, 1)

                    def masked(i, u):
                        b = u % NS
                        at = U * i + u
                        dve.wait_ge(s_sc, at + 1)
                        dve.scalar_tensor_tensor(s[b][:, :], bank[3 + u % 2][:, 0:3 * P], -INV_SCALE,
                                                 cst[:, C_MASK:C_MASK + 3 * P], ALU.mult, ALU.max).then_inc(s_sm, 1)
                        dve.wait_ge(s_sm, at + 1)
                        for t, cols in ((0, slice(0, P)), (1, slice(P, 3 * P))):
                            dve.tensor_reduce(mn[:, b, t:t + 1], s[b][:, cols], op=ALU.min,
                                              axis=AX.X).then_inc(s_mn, 1)

                    def recip(i, u):
                        b = u % NS
                        dve.wait_ge(s_e, 2 * (U * i + u + 1))
                        dve.reciprocal(rr[:, b, :], rs[:, b, :]).then_inc(s_rr, 1)

                    def z_low(i, u):
                        bt, h = unit(u)
                        cols = slice(bt * SEQ, (bt + 1) * SEQ)
                        dve.wait_ge(s_zh, U * i + u + 1)
                        dve.scalar_tensor_tensor(zT_l[:, h, cols], bank[ZB[u % 2]][:, 0:SEQ],
                                                 bias[:, 2, h:h + 1], zT_h[:, h, cols].bitcast(FP32),
                                                 ALU.add, ALU.subtract).then_inc(s_zl, 1)

                    def added(i, bt):
                        dve.wait_ge(s_o, BATCH * i + bt + 1)
                        r = x_res[:, 2 * bt:2 * bt + 2, :].rearrange("p a b -> p (a b)")
                        dve.tensor_tensor(r, r, bank[BANK[f"O{bt}"]][:, :], ALU.add).then_inc(s_ov, 1)

                    def body(i, fresh=False, last=False):
                        dve.wait_ge(s_bp, i + 1)
                        for item in DVE_ORDER:
                            kind, x = item[0], int(item[1])
                            if fresh and item == "K0":
                                dve.wait_ge(s_bo, 16)
                                dve.tensor_tensor(x_res[:, :, :], x_res[:, :, :],
                                                  bo_sb[:, :].unsqueeze(1).to_broadcast([P, NT, D]),
                                                  ALU.add).then_inc(s_bo, 1)
                            if fresh and item == "O0":
                                dve.wait_ge(s_bo, 17)
                            if last and item == "O2":
                                dve.wait_ge(s_ov, BATCH * i + 2)
                                norm_stats(dve, norm3, 0)
                            if kind in "ABV":
                                proj(i, item)
                            elif item == "O3":
                                if fresh:
                                    norm_low(dve, n, 1, (5, 6))
                                else:
                                    added(i - 1, x)
                            else:
                                {"K": masked, "R": recip, "L": z_low, "O": added}[kind](i, x)

                    def next_bias(i):
                        dve.wait_ge(s_zl, U * (i + 1))
                        dve.tensor_copy(bias[:, :, :], bias_all[:, :, bass.ds(2 * i + 2, 2)]).then_inc(s_bp, 1)

                    body(0, True)
                    next_bias(0)
                    with dve.Fori(1, NP - 1) as i:
                        body(i)
                        next_bias(i)
                    body(NP - 1, last=True)
                    added(NP - 1, BATCH - 1)
                    norm_apply(dve, norm3, 0)
                    norm_low(dve, norm3, 0, (3, 4))

                @block.tensor
                def _(pe):
                    def bank_free(i, item, fresh):
                        at = BANKED.index(item)
                        if fresh and at < 2:
                            return
                        if fresh and BANKED[at - 2] == "O3":
                            at -= 2
                        prior = BANKED[at - 2]
                        pair = i if at >= 2 else i - 1
                        if prior[0] == "O":
                            pe.wait_ge(s_ov, BATCH * pair + (int(prior[1]) + 1) % BATCH)
                        elif prior in ON_ACT:
                            pe.wait_ge(s_pa, (PROJ // 2) * pair + ON_ACT.index(prior) + 1)
                        else:
                            pe.wait_ge(s_pv, (PROJ // 2) * pair + ON_DVE.index(prior) + 1)

                    def projected(i, *items):
                        pe.wait_ge(s_pa, (PROJ // 2) * i + max(ON_ACT.index(x) + 1 for x in items if x in ON_ACT))
                        pe.wait_ge(s_pv, (PROJ // 2) * i + max(ON_DVE.index(x) + 1 for x in items if x in ON_DVE))

                    def proj(i, item, fresh):
                        kind, x = item[0], int(item[1])
                        b = bank[BANK[item]]
                        bank_free(i, item, fresh)
                        if kind == "V":
                            for j in range(2):
                                toks = slice((2 * x + j) * P, (2 * x + j + 1) * P)
                                for k in range(KD):
                                    last = split_matmuls(pe, b[:, j * 2 * DH:(j + 1) * 2 * DH],
                                                         (xT_h[:, k, toks], xT_l[:, k, toks]),
                                                         (w_h[:, 2, k, :], w_l[:, 2, k, :]), k == 0, k == KD - 1)
                        else:
                            t, h, half = x // 2, x % 2, "AB".index(kind)
                            toks = slice(half * HALF, (half + 1) * HALF)
                            w = slice(h * DH, (h + 1) * DH)
                            for k in range(KD):
                                last = split_matmuls(pe, b[:, :], (w_h[:, t, k, w], w_l[:, t, k, w]),
                                                     (xT_h[:, k, toks], xT_l[:, k, toks]), k == 0, k == KD - 1)
                        last.then_inc(s_proj, 1)

                    def scores(i, u):
                        bt, h = unit(u)
                        b = bank[3 + u % 2]
                        if u == 0:
                            projected(i, "A0", "A1", "A2", "A3")
                        if u == U // 2:
                            projected(i, "B0", "B1", "B2", "B3")
                        if u >= 2:
                            pe.wait_ge(s_sm, U * i + u - 1)
                        q, k = qk[:, 0, h, :], qk[:, 1, h, :]
                        t0 = bt * SEQ
                        pe.matmul(b[:, 0:P], q[:, t0:t0 + P], k[:, t0:t0 + P], start=True, stop=True)
                        pe.matmul(b[:, P:3 * P], q[:, t0 + P:t0 + 2 * P], k[:, t0:t0 + 2 * P],
                                  start=True, stop=True).then_inc(s_sc, 1)

                    def turn(i, u):
                        pe.wait_ge(s_p, 2 * (U * i + u + 1))
                        if u >= 2:
                            pe.wait_ge(s_ptv, U * i + u - 1)
                        for c in range(3):
                            last = pe.transpose(bank[5 + u % 2][:, c * P:(c + 1) * P],
                                                s[u % NS][:, c * P:(c + 1) * P], ident)
                        last.then_inc(s_pt, 1)

                    def mix(i, u):
                        bt, h = unit(u)
                        pe.wait_ge(s_ptv, U * i + u + 1)
                        if h == 0:
                            item = f"V{bt}"
                            if item in ON_ACT:
                                pe.wait_ge(s_pa, (PROJ // 2) * i + ON_ACT.index(item) + 1)
                            else:
                                pe.wait_ge(s_pv, (PROJ // 2) * i + ON_DVE.index(item) + 1)
                        if u >= 2:
                            pe.wait_ge(s_zl, U * i + u - 1)
                        e = slice(h * DH, (h + 1) * DH)
                        pe.matmul(bank[ZB[u % 2]][:, 0:2 * P], v[:, 2 * bt, e], pT[u % 2][:, 0:2 * P], start=True, stop=False)
                        pe.matmul(bank[ZB[u % 2]][:, P:2 * P], v[:, 2 * bt + 1, e], pT[u % 2][:, 2 * P:3 * P],
                                  start=False, stop=True).then_inc(s_z, 1)

                    def project(i, bt, fresh=False, end=False):
                        pe.wait_ge(s_zh, U * i + 2 * bt + 2)
                        pe.wait_ge(s_zl, U * i + 2 * bt + 2)
                        if bt == 0:
                            pe.wait_ge(s_wol, i + 1)
                        if end:
                            assert BANKED[-2] == "O1" and BANK["O1"] == BANK["O3"]
                            pe.wait_ge(s_ov, BATCH * i + 2)
                        else:
                            bank_free(i + (bt == BATCH - 1), f"O{bt}", fresh)
                        for j in range(2):
                            toks = slice((2 * bt + j) * P, (2 * bt + j + 1) * P)
                            for h in range(2):
                                last = split_matmuls(pe, bank[BANK[f"O{bt}"]][:, j * D:(j + 1) * D],
                                                     (zT_h[:, h, toks], zT_l[:, h, toks]),
                                                     (wo_h[:, h, :], wo_l[:, h, :]), h == 0, h == 1)
                        last.then_inc(s_o, 1)

                    def body(i, fresh):
                        pe.wait_ge(s_ql, 2 * i + 1)
                        for item in ORDER:
                            kind, x = item[0], int(item[1])
                            if fresh and item == "A2":
                                norm_turn(pe, n, 1, (5, 6))
                            if fresh and item == "B0":
                                norm_wait(pe, n, 1)
                            if item == "V0":
                                pe.wait_ge(s_ql, 2 * i + 2)
                            if kind in "ABV":
                                proj(i, item, fresh)
                            elif item == "O3":
                                if not fresh:
                                    project(i - 1, x)
                            else:
                                {"S": scores, "T": turn, "M": mix, "O": project}[kind](i, x)

                    body(0, True)
                    with pe.Fori(1, NP) as i:
                        body(i, False)
                    keep_warm(pe, 4, WARM[4])
                    project(NP - 1, BATCH - 1, end=True)
                    keep_warm(pe, 7, WARM[5])
                    norm_turn(pe, norm3, 0, (3, 4))

                block_ctx.close()

        ffn("f0", True, norm1, norm2)
        attention()
        ffn("f1", False, norm3, None)


def kernel(**inputs):
    import concourse.bacc as bacc
    from concourse.bass_utils import run_bass_kernel_spmd

    def chunks(w, rows, p):
        w = w.reshape(*w.shape[:-2], rows // p, p, w.shape[-1])
        return np.moveaxis(w, -2, 0)

    a = {k.removeprefix("L0_"): np.asarray(v) for k, v in inputs.items()}
    gu = a["ffn_shared_gate_up_w"].reshape(2, ISH, KD, P)
    whole = (SC - 1) * P
    gu = np.concatenate([
        gu[:, :whole].reshape(2, SC - 1, P, KD, P).transpose(4, 1, 0, 3, 2).reshape(P, -1),
        gu[::-1, whole:].transpose(3, 2, 0, 1).reshape(P, -1)], 1)
    dn = np.concatenate([a["ffn_shared_down_w"], np.zeros((D, SC * P - ISH), np.float32)], 1)
    gate = np.concatenate([a["ffn_gate_w"], a["ffn_shared_gate_w"], np.zeros((P - NG, D), np.float32)], 0)

    def heads(w):
        w = w.reshape(NP, 2, KD, P, DH)
        return w.transpose(0, 3, 2, 1, 4)

    arrays = {
        "x_in": a["attn_x"].reshape(TOK, D),
        "consts": constants(),
        "wgate": chunks(gate.T, D, P).reshape(P, KD * P),
        "wgu": gu,
        "wd": chunks(dn.T, SC * P, P),
        "w1": chunks(a["ffn_w1"].transpose(0, 2, 1), D, P),
        "w2": chunks(a["ffn_w2"].transpose(0, 2, 1), IM, IC),
        "wqkv": np.stack([heads(a[f"attn_W_{t}"]) for t in "QKV"], 2).reshape(NP, P, -1),
        "wo": a["attn_W_O"].reshape(NP, 2, DH, D).transpose(0, 2, 1, 3).reshape(NP, P, 2 * D),
        "bqkv": np.stack([a[f"attn_b_{t}"].T for t in "QKV"], 1),
        "bo": a["attn_b_O"],
    }
    nc = bacc.Bacc("TRN2", target_bir_lowering=False, num_devices=1)
    ins, aps = {}, {}
    for name, arr in arrays.items():
        arr = np.ascontiguousarray(arr)
        ins[f"in_{name}"] = arr
        aps[name] = nc.dram_tensor(f"in_{name}", arr.shape, mybir.dt.from_np(arr.dtype), kind="ExternalInput").ap()
    aps["out"] = nc.dram_tensor("out_0", (TOK, D), FP32, kind="ExternalOutput").ap()
    macaron(nc, **aps)
    r = run_bass_kernel_spmd(nc, [ins], core_ids=[0])
    return r.results[0]["out_0"].reshape(BATCH, SEQ, D)
```
